# Optimizing a Trainium2 kernel written in Bass

```python
import numpy as np
import jax
import jax.numpy as jnp

def _softmax(x, axis=-1):
    return jax.nn.softmax(x, axis=axis)

def _gelu(x):
    return jax.nn.gelu(x, approximate=True)

def _silu(x):
    return jax.nn.silu(x)

def _sigmoid(x):
    return jax.nn.sigmoid(x)

def _layernorm(x, axis=-1, eps=1e-05):
    m = jnp.mean(x, axis=axis, keepdims=True)
    v = jnp.var(x, axis=axis, keepdims=True)
    return (x - m) / jnp.sqrt(v + eps)

def _scatter_add(tgt, idx, src, axis=0):
    return tgt.at[idx].add(src)

def _segment_sum(src, seg, n):
    return jax.ops.segment_sum(src, seg, n)
kernel_name = 'mk_dlrm_tower_d1_rec_r8_874bbb'

def setup_inputs(seed: int=0):
    np.random.seed(seed)
    _w = jnp.asarray

    def _rec_inputs():
        import jax
        import jax.numpy as jnp
        _tk = jax.random.key(seed)
        dense_ctx = jax.random.normal(jax.random.fold_in(_tk, 190), (512, 16), jnp.float32)
        ids = jnp.stack([jax.random.randint(jax.random.fold_in(_tk, 200 + f), (512,), 0, v, jnp.int32) for f, v in enumerate([1000, 1250, 12500, 125000, 125000, 1000, 125000, 1250, 1000, 125000, 1250, 12500, 125000, 1250, 12500, 125000, 125000, 1000, 1000, 1250, 1000, 12500, 1250, 1000, 1000, 125000, 1000, 1250, 12500, 12500, 1000, 125000, 1250, 1250, 1250, 125000, 1250, 1000, 1000])], axis=1)
        tbl_0 = 0.05 * jax.random.normal(jax.random.fold_in(_tk, 500 + 0), (1000, 16), jnp.float32)
        tbl_1 = 0.05 * jax.random.normal(jax.random.fold_in(_tk, 500 + 1), (1250, 16), jnp.float32)
        tbl_2 = 0.05 * jax.random.normal(jax.random.fold_in(_tk, 500 + 2), (12500, 16), jnp.float32)
        tbl_3 = 0.05 * jax.random.normal(jax.random.fold_in(_tk, 500 + 3), (125000, 16), jnp.float32)
        tbl_4 = 0.05 * jax.random.normal(jax.random.fold_in(_tk, 500 + 4), (125000, 16), jnp.float32)
        tbl_5 = 0.05 * jax.random.normal(jax.random.fold_in(_tk, 500 + 5), (1000, 16), jnp.float32)
        tbl_6 = 0.05 * jax.random.normal(jax.random.fold_in(_tk, 500 + 6), (125000, 16), jnp.float32)
        tbl_7 = 0.05 * jax.random.normal(jax.random.fold_in(_tk, 500 + 7), (1250, 16), jnp.float32)
        tbl_8 = 0.05 * jax.random.normal(jax.random.fold_in(_tk, 500 + 8), (1000, 16), jnp.float32)
        tbl_9 = 0.05 * jax.random.normal(jax.random.fold_in(_tk, 500 + 9), (125000, 16), jnp.float32)
        tbl_10 = 0.05 * jax.random.normal(jax.random.fold_in(_tk, 500 + 10), (1250, 16), jnp.float32)
        tbl_11 = 0.05 * jax.random.normal(jax.random.fold_in(_tk, 500 + 11), (12500, 16), jnp.float32)
        tbl_12 = 0.05 * jax.random.normal(jax.random.fold_in(_tk, 500 + 12), (125000, 16), jnp.float32)
        tbl_13 = 0.05 * jax.random.normal(jax.random.fold_in(_tk, 500 + 13), (1250, 16), jnp.float32)
        tbl_14 = 0.05 * jax.random.normal(jax.random.fold_in(_tk, 500 + 14), (12500, 16), jnp.float32)
        tbl_15 = 0.05 * jax.random.normal(jax.random.fold_in(_tk, 500 + 15), (125000, 16), jnp.float32)
        tbl_16 = 0.05 * jax.random.normal(jax.random.fold_in(_tk, 500 + 16), (125000, 16), jnp.float32)
        tbl_17 = 0.05 * jax.random.normal(jax.random.fold_in(_tk, 500 + 17), (1000, 16), jnp.float32)
        tbl_18 = 0.05 * jax.random.normal(jax.random.fold_in(_tk, 500 + 18), (1000, 16), jnp.float32)
        tbl_19 = 0.05 * jax.random.normal(jax.random.fold_in(_tk, 500 + 19), (1250, 16), jnp.float32)
        tbl_20 = 0.05 * jax.random.normal(jax.random.fold_in(_tk, 500 + 20), (1000, 16), jnp.float32)
        tbl_21 = 0.05 * jax.random.normal(jax.random.fold_in(_tk, 500 + 21), (12500, 16), jnp.float32)
        tbl_22 = 0.05 * jax.random.normal(jax.random.fold_in(_tk, 500 + 22), (1250, 16), jnp.float32)
        tbl_23 = 0.05 * jax.random.normal(jax.random.fold_in(_tk, 500 + 23), (1000, 16), jnp.float32)
        tbl_24 = 0.05 * jax.random.normal(jax.random.fold_in(_tk, 500 + 24), (1000, 16), jnp.float32)
        tbl_25 = 0.05 * jax.random.normal(jax.random.fold_in(_tk, 500 + 25), (125000, 16), jnp.float32)
        tbl_26 = 0.05 * jax.random.normal(jax.random.fold_in(_tk, 500 + 26), (1000, 16), jnp.float32)
        tbl_27 = 0.05 * jax.random.normal(jax.random.fold_in(_tk, 500 + 27), (1250, 16), jnp.float32)
        tbl_28 = 0.05 * jax.random.normal(jax.random.fold_in(_tk, 500 + 28), (12500, 16), jnp.float32)
        tbl_29 = 0.05 * jax.random.normal(jax.random.fold_in(_tk, 500 + 29), (12500, 16), jnp.float32)
        tbl_30 = 0.05 * jax.random.normal(jax.random.fold_in(_tk, 500 + 30), (1000, 16), jnp.float32)
        tbl_31 = 0.05 * jax.random.normal(jax.random.fold_in(_tk, 500 + 31), (125000, 16), jnp.float32)
        tbl_32 = 0.05 * jax.random.normal(jax.random.fold_in(_tk, 500 + 32), (1250, 16), jnp.float32)
        tbl_33 = 0.05 * jax.random.normal(jax.random.fold_in(_tk, 500 + 33), (1250, 16), jnp.float32)
        tbl_34 = 0.05 * jax.random.normal(jax.random.fold_in(_tk, 500 + 34), (1250, 16), jnp.float32)
        tbl_35 = 0.05 * jax.random.normal(jax.random.fold_in(_tk, 500 + 35), (125000, 16), jnp.float32)
        tbl_36 = 0.05 * jax.random.normal(jax.random.fold_in(_tk, 500 + 36), (1250, 16), jnp.float32)
        tbl_37 = 0.05 * jax.random.normal(jax.random.fold_in(_tk, 500 + 37), (1000, 16), jnp.float32)
        tbl_38 = 0.05 * jax.random.normal(jax.random.fold_in(_tk, 500 + 38), (1000, 16), jnp.float32)
        _rk = jax.random.fold_in(_tk, 7)
        W_top1 = 0.0606339 * jax.random.normal(jax.random.fold_in(_tk, 801), (272, 512), jnp.float32)
        W_top2 = 0.0441942 * jax.random.normal(jax.random.fold_in(_tk, 802), (512, 256), jnp.float32)
        W_top3 = 0.0625 * jax.random.normal(jax.random.fold_in(_tk, 803), (256, 1), jnp.float32)
        b_top1 = jnp.zeros((512,), jnp.float32)
        b_top2 = jnp.zeros((256,), jnp.float32)
        return (dense_ctx, ids, tbl_0, tbl_1, tbl_2, tbl_3, tbl_4, tbl_5, tbl_6, tbl_7, tbl_8, tbl_9, tbl_10, tbl_11, tbl_12, tbl_13, tbl_14, tbl_15, tbl_16, tbl_17, tbl_18, tbl_19, tbl_20, tbl_21, tbl_22, tbl_23, tbl_24, tbl_25, tbl_26, tbl_27, tbl_28, tbl_29, tbl_30, tbl_31, tbl_32, tbl_33, tbl_34, tbl_35, tbl_36, tbl_37, tbl_38, W_top1, b_top1, W_top2, b_top2, W_top3)
    dense_ctx, ids, tbl_0, tbl_1, tbl_2, tbl_3, tbl_4, tbl_5, tbl_6, tbl_7, tbl_8, tbl_9, tbl_10, tbl_11, tbl_12, tbl_13, tbl_14, tbl_15, tbl_16, tbl_17, tbl_18, tbl_19, tbl_20, tbl_21, tbl_22, tbl_23, tbl_24, tbl_25, tbl_26, tbl_27, tbl_28, tbl_29, tbl_30, tbl_31, tbl_32, tbl_33, tbl_34, tbl_35, tbl_36, tbl_37, tbl_38, W_top1, b_top1, W_top2, b_top2, W_top3 = _rec_inputs()

    def _L0_rec_setup():
        import jax, jax.numpy as jnp
        import numpy as np
        B, F, D = (1024, 39, 16)
        HIDDEN = [128, 128, 128]

        def _cin(x, Ws, bs):
            F0 = x.shape[1]
            h = x
            outs = []
            n = len(Ws)
            for i, (W, b) in enumerate(zip(Ws, bs)):
                L = W.shape[-1]
                Fk = h.shape[1]
                Wr = W.reshape(F0, Fk, L)
                z = jnp.einsum('bfd,bgd->bfgd', x, h)
                cur = jax.nn.relu(jnp.einsum('bfgd,fgl->bld', z, Wr) + b[None, :, None])
                if i != n - 1:
                    h = cur[:, :L // 2]
                    direct = cur[:, L // 2:]
                else:
                    direct = cur
                outs.append(direct)
            return jnp.concatenate(outs, axis=1).sum(-1)
        key = jax.random.key(seed)
        ks = jax.random.split(key, 8)
        x = jax.random.normal(ks[0], (B, F, D), dtype=jnp.float32)
        field_nums = [F]
        Ws, bs = ([], [])
        for i, L in enumerate(HIDDEN):
            fan_in = field_nums[0] * field_nums[-1]
            lim = np.sqrt(6.0 / fan_in)
            Ws.append(jax.random.uniform(ks[1 + i], (fan_in, L), jnp.float32, -lim, lim))
            bs.append(jnp.zeros((L,), jnp.float32))
            field_nums.append(L // 2)
        return {'x': x, 'W0': Ws[0], 'W1': Ws[1], 'W2': Ws[2], 'b0': bs[0], 'b1': bs[1], 'b2': bs[2]}
    _L0_rec_all = _L0_rec_setup()
    _L0_rec_in = {k: v for k, v in _L0_rec_all.items() if k in ('W0', 'W1', 'W2', 'b0', 'b1', 'b2')}
    del _L0_rec_all
    return {'dense_ctx': dense_ctx, 'ids': ids, 'tbl_0': tbl_0, 'tbl_1': tbl_1, 'tbl_2': tbl_2, 'tbl_3': tbl_3, 'tbl_4': tbl_4, 'tbl_5': tbl_5, 'tbl_6': tbl_6, 'tbl_7': tbl_7, 'tbl_8': tbl_8, 'tbl_9': tbl_9, 'tbl_10': tbl_10, 'tbl_11': tbl_11, 'tbl_12': tbl_12, 'tbl_13': tbl_13, 'tbl_14': tbl_14, 'tbl_15': tbl_15, 'tbl_16': tbl_16, 'tbl_17': tbl_17, 'tbl_18': tbl_18, 'tbl_19': tbl_19, 'tbl_20': tbl_20, 'tbl_21': tbl_21, 'tbl_22': tbl_22, 'tbl_23': tbl_23, 'tbl_24': tbl_24, 'tbl_25': tbl_25, 'tbl_26': tbl_26, 'tbl_27': tbl_27, 'tbl_28': tbl_28, 'tbl_29': tbl_29, 'tbl_30': tbl_30, 'tbl_31': tbl_31, 'tbl_32': tbl_32, 'tbl_33': tbl_33, 'tbl_34': tbl_34, 'tbl_35': tbl_35, 'tbl_36': tbl_36, 'tbl_37': tbl_37, 'tbl_38': tbl_38, 'W_top1': W_top1, 'b_top1': b_top1, 'W_top2': W_top2, 'b_top2': b_top2, 'W_top3': W_top3, 'L0_rec_W0': _L0_rec_in['W0'], 'L0_rec_W1': _L0_rec_in['W1'], 'L0_rec_W2': _L0_rec_in['W2'], 'L0_rec_b0': _L0_rec_in['b0'], 'L0_rec_b1': _L0_rec_in['b1'], 'L0_rec_b2': _L0_rec_in['b2']}

def reference(dense_ctx, ids, tbl_0, tbl_1, tbl_2, tbl_3, tbl_4, tbl_5, tbl_6, tbl_7, tbl_8, tbl_9, tbl_10, tbl_11, tbl_12, tbl_13, tbl_14, tbl_15, tbl_16, tbl_17, tbl_18, tbl_19, tbl_20, tbl_21, tbl_22, tbl_23, tbl_24, tbl_25, tbl_26, tbl_27, tbl_28, tbl_29, tbl_30, tbl_31, tbl_32, tbl_33, tbl_34, tbl_35, tbl_36, tbl_37, tbl_38, W_top1, b_top1, W_top2, b_top2, W_top3, L0_rec_W0, L0_rec_W1, L0_rec_W2, L0_rec_b0, L0_rec_b1, L0_rec_b2):
    import jax
    import jax.numpy as jnp

    def _L0_rec_ref(x, W0, W1, W2, b0, b1, b2):
        import jax, jax.numpy as jnp
        import numpy as np
        B, F, D = (1024, 39, 16)
        HIDDEN = [128, 128, 128]

        def _cin(x, Ws, bs):
            F0 = x.shape[1]
            h = x
            outs = []
            n = len(Ws)
            for i, (W, b) in enumerate(zip(Ws, bs)):
                L = W.shape[-1]
                Fk = h.shape[1]
                Wr = W.reshape(F0, Fk, L)
                z = jnp.einsum('bfd,bgd->bfgd', x, h)
                cur = jax.nn.relu(jnp.einsum('bfgd,fgl->bld', z, Wr) + b[None, :, None])
                if i != n - 1:
                    h = cur[:, :L // 2]
                    direct = cur[:, L // 2:]
                else:
                    direct = cur
                outs.append(direct)
            return jnp.concatenate(outs, axis=1).sum(-1)
        return _cin(x, [W0, W1, W2], [b0, b1, b2])
    e = jnp.stack([tbl_0[ids[:, 0]], tbl_1[ids[:, 1]], tbl_2[ids[:, 2]], tbl_3[ids[:, 3]], tbl_4[ids[:, 4]], tbl_5[ids[:, 5]], tbl_6[ids[:, 6]], tbl_7[ids[:, 7]], tbl_8[ids[:, 8]], tbl_9[ids[:, 9]], tbl_10[ids[:, 10]], tbl_11[ids[:, 11]], tbl_12[ids[:, 12]], tbl_13[ids[:, 13]], tbl_14[ids[:, 14]], tbl_15[ids[:, 15]], tbl_16[ids[:, 16]], tbl_17[ids[:, 17]], tbl_18[ids[:, 18]], tbl_19[ids[:, 19]], tbl_20[ids[:, 20]], tbl_21[ids[:, 21]], tbl_22[ids[:, 22]], tbl_23[ids[:, 23]], tbl_24[ids[:, 24]], tbl_25[ids[:, 25]], tbl_26[ids[:, 26]], tbl_27[ids[:, 27]], tbl_28[ids[:, 28]], tbl_29[ids[:, 29]], tbl_30[ids[:, 30]], tbl_31[ids[:, 31]], tbl_32[ids[:, 32]], tbl_33[ids[:, 33]], tbl_34[ids[:, 34]], tbl_35[ids[:, 35]], tbl_36[ids[:, 36]], tbl_37[ids[:, 37]], tbl_38[ids[:, 38]]], axis=1)
    z = _L0_rec_ref(e, L0_rec_W0, L0_rec_W1, L0_rec_W2, L0_rec_b0, L0_rec_b1, L0_rec_b2)
    z = z.reshape(z.shape[0], -1)
    h = jnp.concatenate([z, dense_ctx], axis=1)
    h = jnp.maximum(h @ W_top1 + b_top1, 0.0)
    h = jnp.maximum(h @ W_top2 + b_top2, 0.0)
    y = h @ W_top3
    return y

_drawn_inputs = setup_inputs


def setup_inputs(seed=0):
    import zlib

    import numpy as np

    out = dict(_drawn_inputs(seed))
    spreads = {'b_top1': (0.0, 2.0),
     'b_top2': (0.0, 2.0),
     'L0_rec_b0': (0.0, 0.325),
     'L0_rec_b1': (0.0, 0.448),
     'L0_rec_b2': (0.0, 0.8)}
    factors = {'tbl_0': 8.0,
     'tbl_1': 8.0,
     'tbl_2': 8.0,
     'tbl_3': 8.0,
     'tbl_4': 8.0,
     'tbl_5': 8.0,
     'tbl_6': 8.0,
     'tbl_7': 8.0,
     'tbl_8': 8.0,
     'tbl_9': 8.0,
     'tbl_10': 8.0,
     'tbl_11': 8.0,
     'tbl_12': 8.0,
     'tbl_13': 8.0,
     'tbl_14': 8.0,
     'tbl_15': 8.0,
     'tbl_16': 8.0,
     'tbl_17': 8.0,
     'tbl_18': 8.0,
     'tbl_19': 8.0,
     'tbl_20': 8.0,
     'tbl_21': 8.0,
     'tbl_22': 8.0,
     'tbl_23': 8.0,
     'tbl_24': 8.0,
     'tbl_25': 8.0,
     'tbl_26': 8.0,
     'tbl_27': 8.0,
     'tbl_28': 8.0,
     'tbl_29': 8.0,
     'tbl_30': 8.0,
     'tbl_31': 8.0,
     'tbl_32': 8.0,
     'tbl_33': 8.0,
     'tbl_34': 8.0,
     'tbl_35': 8.0,
     'tbl_36': 8.0,
     'tbl_37': 8.0,
     'tbl_38': 8.0,
     'L0_rec_W0': 8.0,
     'L0_rec_W1': 5.376,
     'L0_rec_W2': 4.767,
     'dense_ctx': 8.0}
    for name, (base, spread) in spreads.items():
        noise = np.random.default_rng([zlib.crc32(name.encode()), seed]).standard_normal(out[name].shape)
        drawn = base * np.exp(spread * noise) if base else spread * noise
        out[name] = jnp.asarray(drawn.astype(out[name].dtype))
    for name, factor in factors.items():
        out[name] = (out[name] * factor).astype(out[name].dtype)
    return out
```

```python
import concourse.bass as bass
from concourse import mybir
from contextlib import ExitStack

BATCH, FIELDS, DIM = 512, 39, 16
CHANNELS = 128
HIDDEN = CHANNELS // 2
DENSE, TOP1, TOP2 = 16, 512, 256
P = 128

CHUNK_B = 32
COLS = CHUNK_B * DIM
CHUNKS = BATCH // CHUNK_B

LANES = P // CHUNK_B
GATHERS = -(-FIELDS // LANES)
LAST_LANES = FIELDS - (GATHERS - 1) * LANES

DISTS = FIELDS // 2 + 1
PER_TILE = P // FIELDS
TILES0 = -(-DISTS // PER_TILE)
ROWS0 = PER_TILE * FIELDS
LAST_ROWS0 = (DISTS - (TILES0 - 1) * PER_TILE) * FIELDS
WRAP_GATHERS = 5
WRAP = WRAP_GATHERS * LANES
ROWS_X = FIELDS + WRAP

TILES = -(-FIELDS // 2)
GROUP = 4
GROUPS0 = [4, 3]
GROUPS1 = [4] * 5
RING = 4
PER_STEP = len(GROUPS0) + 2 * len(GROUPS1)
assert PER_STEP % RING == 0 and sum(GROUPS0) == TILES0 and sum(GROUPS1) == TILES

F32 = mybir.dt.float32
I32 = mybir.dt.int32
ALU = mybir.AluOpType
ACT = mybir.ActivationFunctionType
AX = mybir.AxisListType


def groups_done(step, layers):
    within = [0, len(GROUPS1), len(GROUPS1) + len(GROUPS0), PER_STEP][layers]
    return step * PER_STEP + len(GROUPS0) + within


def before(c, n):
    return isinstance(c, int) and c < n


def last(c):
    return isinstance(c, int) and c == CHUNKS - 1


def build(nc, ids, bases, table, w0a, w0b, w1, w2, cin_b, dense, wt1, wt2, wt3, bt1, bt2, out):
    ctx = ExitStack()
    with ctx:
        def sb(name, shape, dt=F32):
            return ctx.enter_context(nc.sbuf_tensor(name, shape, dt))

        def pb(name, shape=(P, COLS)):
            return ctx.enter_context(nc.psum_tensor(name, list(shape), F32))

        def sem(name):
            return ctx.enter_context(nc.semaphore(name))

        ids_sb = sb("ids_sb", [P, CHUNKS * GATHERS], I32)
        bases_sb = sb("bases_sb", [P, CHUNKS * GATHERS], I32)
        rows_all = sb("rows_all", [P, CHUNKS * GATHERS], I32)
        rows_now = sb("rows_now", [P, 2, GATHERS], I32)
        looked_up = sb("looked_up", [P, 2, GATHERS, DIM])
        x_dram = nc.dram_tensor("x_scratch", (CHUNKS * ROWS_X, COLS), F32, kind="Internal").ap()
        pair_x = sb("pair_x", [ROWS0, TILES0 + 1, COLS])
        field_x = sb("field_x", [P, 2, TILES, COLS])
        products = sb("products", [P, RING, GROUP, COLS])
        w0_sb = sb("w0_sb", [ROWS0, TILES0, CHANNELS])
        w0b_sb = sb("w0b_sb", [ROWS0, TILES0, CHANNELS])
        w1_sb = sb("w1_sb", [P, TILES, CHANNELS])
        w2_sb = sb("w2_sb", [P, TILES, CHANNELS])
        cin_b_sb = sb("cin_b_sb", [P, 3])
        direct = sb("direct", [P, 2, 2, COLS])
        z_sb = sb("z_sb", [P, 2, BATCH])
        dense_sb = sb("dense_sb", [DENSE, BATCH])
        wt1_sb = sb("wt1_sb", [P, 2, TOP1])
        wt1d_sb = sb("wt1d_sb", [DENSE, TOP1])
        wt2_sb = sb("wt2_sb", [P, TOP1 // P, TOP2])
        wt3_sb = sb("wt3_sb", [P, TOP2 // P])
        bt1_sb = sb("bt1_sb", [P, TOP1 // P])
        bt2_sb = sb("bt2_sb", [P, TOP2 // P])
        top1_sb = sb("top1_sb", [P, TOP1 // P, BATCH])
        top2_sb = sb("top2_sb", [P, TOP2 // P, BATCH])
        y_sb = sb("y_sb", [1, BATCH])

        acc = [pb(f"acc{layer}") for layer in range(3)]
        hidden = [pb("hidden1"), pb("hidden2")]
        top_acc = [pb("top_acc0"), pb("top_acc1")]

        pool_passed = sem("pool_passed")
        sp_passed = sem("sp_passed")
        rows_loaded = sem("rows_loaded")
        rows_added = sem("rows_added")
        rows_ready = sem("rows_ready")
        gathered = [sem("gathered0"), sem("gathered1")]
        x_stored = [sem("x_stored0"), sem("x_stored1")]
        pair_x_loaded = sem("pair_x_loaded")
        field_x_head = [sem("field_x_head0"), sem("field_x_head1")]
        field_x_rest = [sem("field_x_rest0"), sem("field_x_rest1")]
        pads_zeroed = sem("pads_zeroed")
        w0_loaded = sem("w0_loaded")
        w0_folded = sem("w0_folded")
        w1_loaded = sem("w1_loaded")
        w2_loaded = sem("w2_loaded")
        biases_loaded = sem("biases_loaded")
        top_loaded = sem("top_loaded")
        products_ready = sem("products_ready")
        products_used = sem("products_used")
        hidden_ready = [sem("hidden1_ready"), sem("hidden2_ready")]
        acc_drained = [sem(f"acc{layer}_drained") for layer in range(3)]
        z_summed = sem("z_summed")
        top1_done = sem("top1_done")
        top1_ready = sem("top1_ready")
        top2_done = sem("top2_done")
        top2_ready = sem("top2_ready")
        y_done = sem("y_done")
        y_ready = sem("y_ready")
        y_stored = sem("y_stored")

        def steps(engine, step):
            step(0, 0)
            step(1, 1)
            with engine.Fori(1, CHUNKS // 2 - 1) as i:
                step(2 * i, 0)
                step(2 * i + 1, 1)
            step(CHUNKS - 2, 0)
            step(CHUNKS - 1, 1)

        STORE_INC = 16 * 2 * LANES
        HALVES = 2
        HEAD = GROUPS1[0]

        block = ctx.enter_context(nc.Block())

        @block.gpsimd
        def _(pool):
            pool.wait_ge(rows_loaded, 32)
            nc.gpsimd.tensor_tensor(rows_all[:], ids_sb[:], bases_sb[:], ALU.add).then_inc(rows_added, 1)
            pool.wait_ge(rows_added, 1)

            def gather(c, u, turn):
                if not before(c, 2):
                    pool.wait_ge(x_stored[u], turn * STORE_INC)
                nc.gpsimd.tensor_copy(rows_now[:, u], rows_all[:, bass.ds(c * GATHERS, GATHERS)]
                                      ).then_inc(rows_ready, 1)
                pool.wait_ge(rows_ready, c + 1)
                pool.sem_inc(pool_passed, 1)
                for j in range(GATHERS):
                    n = P if j < GATHERS - 1 else LAST_LANES * CHUNK_B
                    pool.indirect_dma_start(
                        looked_up[0:n, u, j], None, table,
                        bass.IndirectOffsetOnAxis(ap=rows_now[0:n, u, j:j + 1], axis=0),
                    ).then_inc(gathered[u], 16)

            gather(0, 0, 0)
            gather(1, 1, 0)
            with pool.Fori(1, CHUNKS // 2) as i:
                gather(2 * i, 0, i)
                gather(2 * i + 1, 1, i)

        @block.sync
        def _(sp):
            def wait_counted(semaphore, value):
                sp.wait_ge(semaphore, value)
                sp.sem_inc(sp_passed, 1)

            def store_x(c, u, turn):
                wait_counted(gathered[u], (turn + 1) * 16 * GATHERS)
                for first_row, gathers in ((0, GATHERS), (FIELDS, WRAP_GATHERS)):
                    for lane in range(LANES):
                        n = gathers - (gathers == GATHERS and lane >= LAST_LANES)
                        dst = bass.AP(x_dram.tensor, (c * ROWS_X + first_row + lane) * COLS,
                                      [[DIM, CHUNK_B], [LANES * COLS, n], [1, DIM]])
                        sp.dma_start(dst, looked_up[lane * CHUNK_B:(lane + 1) * CHUNK_B, u, 0:n, :]
                                     ).then_inc(x_stored[u], 16)

            def load_pair_x(c, u, turn):
                wait_counted(x_stored[u], (turn + 1) * STORE_INC)
                for i in range(PER_TILE):
                    src = bass.AP(x_dram.tensor, (c * ROWS_X + i) * COLS,
                                  [[COLS, FIELDS], [PER_TILE * COLS, TILES0], [1, COLS]])
                    sp.dma_start(pair_x[i * FIELDS:(i + 1) * FIELDS, 0:TILES0], src
                                 ).then_inc(pair_x_loaded, 16)
                    src = bass.AP(x_dram.tensor, c * ROWS_X * COLS, [[COLS, FIELDS], [1, COLS]])
                    sp.dma_start(pair_x[i * FIELDS:(i + 1) * FIELDS, TILES0], src
                                 ).then_inc(pair_x_loaded, 16)

            def load_field_x(c, u):
                for t0, t1, loaded in ((0, HEAD, field_x_head[u]), (HEAD, TILES, field_x_rest[u])):
                    for half in range(HALVES):
                        n = min(t1, (FIELDS + 1 - half) // 2) - t0
                        src = bass.AP(x_dram.tensor, (c * ROWS_X + 2 * t0 + half) * COLS,
                                      [[0, HIDDEN], [2 * COLS, n], [1, COLS]])
                        sp.dma_start(field_x[half * HIDDEN:(half + 1) * HIDDEN, u, t0:t0 + n], src
                                     ).then_inc(loaded, 16)

            store_x(0, 0, 0)
            load_pair_x(0, 0, 0)
            load_field_x(0, 0)
            store_x(1, 1, 0)
            sp.wait_ge(products_ready, groups_done(0, 0))
            load_pair_x(1, 1, 0)

            def step(c, u):
                if not before(c, 1):
                    wait_counted(products_ready, groups_done(c - 1, 3))
                if before(c, CHUNKS - 1):
                    load_field_x(c + 1, 1 - u)
                elif not isinstance(c, int):
                    load_field_x(c + 1, 1 - u)
                if before(c, CHUNKS - 2) or not isinstance(c, int):
                    turn = (c + 2 - u) // 2 if isinstance(c, int) else turn_of[0] + 1
                    store_x(c + 2, u, turn)
                    wait_counted(products_ready, groups_done(c, 2))
                    load_pair_x(c + 2, u, turn)

            turn_of = [None]
            step(0, 0)
            step(1, 1)
            with sp.Fori(1, CHUNKS // 2 - 1) as i:
                turn_of[0] = i
                step(2 * i, 0)
                step(2 * i + 1, 1)
            step(CHUNKS - 2, 0)
            step(CHUNKS - 1, 1)
            sp.wait_ge(y_ready, 1)
            sp.dma_start(out.rearrange("b o -> o b"), y_sb[:]).then_inc(y_stored, 16)
            sp.wait_ge(y_stored, 16)

        @block.scalar
        def _(act):
            act.dma_start(ids_sb[:], ids).then_inc(rows_loaded, 16)
            act.dma_start(bases_sb[:], bases).then_inc(rows_loaded, 16)
            act.dma_start(w0_sb[:], w0a).then_inc(w0_loaded, 16)
            act.dma_start(w0b_sb[:], w0b).then_inc(w0_loaded, 16)
            act.dma_start(cin_b_sb[:], cin_b).then_inc(biases_loaded, 16)
            for w, w_sb, loaded in ((w1, w1_sb, w1_loaded), (w2, w2_sb, w2_loaded)):
                full = (TILES - 1) * P
                act.dma_start(w_sb[:, 0:TILES - 1], w[0:full].rearrange("(t p) l -> p t l", p=P)
                              ).then_inc(loaded, 16)
                act.dma_start(w_sb[0:HIDDEN, TILES - 1], w[full:full + HIDDEN]).then_inc(loaded, 16)
            act.dma_start(wt1_sb[:], wt1[0:2 * P].rearrange("(t p) n -> p t n", p=P)).then_inc(top_loaded, 16)
            act.dma_start(wt1d_sb[:], wt1[2 * P:2 * P + DENSE]).then_inc(top_loaded, 16)
            act.dma_start(wt2_sb[:], wt2.rearrange("(t p) n -> p t n", p=P)).then_inc(top_loaded, 16)
            act.dma_start(wt3_sb[:], wt3).then_inc(top_loaded, 16)
            act.dma_start(bt1_sb[:], bt1).then_inc(top_loaded, 16)
            act.dma_start(bt2_sb[:], bt2).then_inc(top_loaded, 16)
            act.dma_start(dense_sb[:], dense).then_inc(top_loaded, 16)
            act.wait_ge(biases_loaded, 16)

            def relu(dst, src, bias):
                return nc.scalar.activation(dst, src, ACT.Relu, bias=bias)

            def to_hidden(layer):
                lo = slice(0, HIDDEN)
                relu(hidden[layer][lo], acc[layer][lo], cin_b_sb[lo, layer:layer + 1])
                relu(hidden[layer][HIDDEN:P], acc[layer][lo], cin_b_sb[lo, layer:layer + 1]
                     ).then_inc(hidden_ready[layer], 1)

            def to_direct(layer, dst):
                hi = slice(HIDDEN, P)
                relu(dst, acc[layer][hi], cin_b_sb[hi, layer:layer + 1]).then_inc(acc_drained[layer], 1)

            def finish_layer0(c, u):
                to_hidden(0)
                if not before(c, 2):
                    act.wait_ge(z_summed, c - 1)
                to_direct(0, direct[0:HIDDEN, u, 0])

            act.wait_ge(products_used, groups_done(0, 0))
            finish_layer0(0, 0)

            def step(c, u):
                act.wait_ge(products_used, groups_done(c, 1))
                to_hidden(1)
                to_direct(1, direct[HIDDEN:P, u, 0])
                if not before(c, CHUNKS) or before(c, CHUNKS - 1):
                    act.wait_ge(products_used, groups_done(c, 2))
                    finish_layer0(c + 1, 1 - u)
                act.wait_ge(products_used, groups_done(c, 3) - (len(GROUPS0) if last(c) else 0))
                relu(direct[:, u, 1], acc[2][:], cin_b_sb[:, 2:3]).then_inc(acc_drained[2], 1)

            steps(act, step)
            act.wait_ge(top_loaded, 7 * 16)
            for m in range(TOP1 // P):
                act.wait_ge(top1_done, m + 1)
                relu(top1_sb[:, m], top_acc[m % 2][:], bt1_sb[:, m:m + 1]).then_inc(top1_ready, 1)
            for m in range(TOP2 // P):
                act.wait_ge(top2_done, m + 1)
                relu(top2_sb[:, m], top_acc[m % 2][:], bt2_sb[:, m:m + 1]).then_inc(top2_ready, 1)
            act.wait_ge(y_done, 1)
            nc.scalar.activation(y_sb[:], top_acc[0][0:1], ACT.Copy).then_inc(y_ready, 1)

        @block.vector
        def _(dve):
            upper = slice(HIDDEN, P)
            for u in range(2):
                nc.vector.memset(field_x[upper, u, TILES - 1], 0.0).then_inc(pads_zeroed, 1)
            nc.vector.memset(w1_sb[upper, TILES - 1], 0.0).then_inc(pads_zeroed, 1)
            nc.vector.memset(w2_sb[upper, TILES - 1], 0.0).then_inc(pads_zeroed, 1)
            dve.wait_ge(pads_zeroed, 4)
            dve.wait_ge(w0_loaded, 32)
            nc.vector.tensor_tensor(w0_sb[:], w0_sb[:], w0b_sb[:], ALU.add).then_inc(w0_folded, 1)

            def slot_free(step, layers, g, total):
                n = groups_done(step, layers) + g
                if not before(n, RING):
                    dve.wait_ge(products_used, n - RING + 1)
                return (len(GROUPS0) + (groups_done(0, layers) - groups_done(0, 0)) + g) % RING

            def products0(c, slots):
                dve.wait_ge(pair_x_loaded, (c + 1) * 2 * PER_TILE * 16)
                t = 0
                for g, n in enumerate(GROUPS0):
                    s = slots(g)
                    one = pair_x[:, TILES0].unsqueeze(1).to_broadcast([ROWS0, n, COLS])
                    nc.vector.tensor_tensor(products[0:ROWS0, s, 0:n], pair_x[:, t:t + n], one, ALU.mult
                                            ).then_inc(products_ready, 1)
                    t += n

            def products12(layer, c, u, turn, slots):
                if layer == 1:
                    dve.wait_ge(field_x_head[u], (turn + 1) * HALVES * 16)
                dve.wait_ge(hidden_ready[layer - 1], c + 1)
                t = 0
                for g, n in enumerate(GROUPS1):
                    if layer == 1 and g == 1:
                        dve.wait_ge(field_x_rest[u], (turn + 1) * HALVES * 16)
                    s = slots(g)
                    h = hidden[layer - 1][:].unsqueeze(1).to_broadcast([P, n, COLS])
                    nc.vector.tensor_tensor(products[:, s, 0:n], field_x[:, u, t:t + n], h, ALU.mult
                                            ).then_inc(products_ready, 1)
                    t += n

            def sum_components(c, u):
                dve.wait_ge(acc_drained[2], c + 1)
                nc.vector.tensor_reduce(
                    out=z_sb[:, :, bass.ds(c * CHUNK_B, CHUNK_B)],
                    in_=direct[:, u].rearrange("p k (b d) -> p k b d", d=DIM),
                    axis=AX.X, op=ALU.add).then_inc(z_summed, 1)

            for g in range(1):
                products0(0, lambda g: g)

            turn_of = [0]

            def step(c, u):
                products12(1, c, u, turn_of[0], lambda g: slot_free(c, 0, g, None))
                if not before(c, 1):
                    sum_components(c - 1, 1 - u)
                if not last(c):
                    products0(c + 1, lambda g: slot_free(c, 1, g, None))
                    products12(2, c, u, turn_of[0], lambda g: slot_free(c, 2, g, None))
                else:
                    products12(2, c, u, turn_of[0], lambda g: slot_free(c, 1, g, None))

            step(0, 0)
            step(1, 1)
            with dve.Fori(1, CHUNKS // 2 - 1) as i:
                turn_of[0] = i
                step(2 * i, 0)
                step(2 * i + 1, 1)
            turn_of[0] = CHUNKS // 2 - 1
            step(CHUNKS - 2, 0)
            step(CHUNKS - 1, 1)
            sum_components(CHUNKS - 1, 1)

        @block.tensor
        def _(pe):
            w_sb = (w0_sb, w1_sb, w2_sb)

            def contract(layer, step, layers, c):
                if not before(c, 1):
                    pe.wait_ge(acc_drained[layer], c)
                sizes = GROUPS1 if layer else GROUPS0
                t = 0
                for g, n in enumerate(sizes):
                    pe.wait_ge(products_ready, groups_done(step, layers) + g + 1)
                    s = (groups_done(0, layers) + g) % RING
                    for k in range(n):
                        rows = P if layer else (LAST_ROWS0 if t == TILES0 - 1 else ROWS0)
                        done = nc.tensor.matmul(acc[layer][:], w_sb[layer][0:rows, t], products[0:rows, s, k],
                                                start=(t == 0), stop=(t == sum(sizes) - 1))
                        t += 1
                    done.then_inc(products_used, 1)

            pe.wait_ge(w0_folded, 1)
            t = 0
            for g, n in enumerate(GROUPS0):
                pe.wait_ge(products_ready, g + 1)
                for k in range(n):
                    rows = LAST_ROWS0 if t == TILES0 - 1 else ROWS0
                    done = nc.tensor.matmul(acc[0][:], w0_sb[0:rows, t], products[0:rows, g, k],
                                            start=(t == 0), stop=(t == TILES0 - 1))
                    t += 1
                done.then_inc(products_used, 1)
            pe.wait_ge(pads_zeroed, 4)
            pe.wait_ge(w1_loaded, 32)

            def step(c, u):
                contract(1, c, 0, c)
                if not last(c):
                    contract(0, c, 1, c + 1)
                if before(c, 1):
                    pe.wait_ge(w2_loaded, 32)
                contract(2, c, 1 if last(c) else 2, c)

            steps(pe, step)

            pe.wait_ge(top_loaded, 7 * 16)
            pe.wait_ge(z_summed, CHUNKS)
            for m in range(TOP1 // P):
                cols = slice(m * P, (m + 1) * P)
                if m >= 2:
                    pe.wait_ge(top1_ready, m - 1)
                nc.tensor.matmul(top_acc[m % 2][:], wt1_sb[:, 0, cols], z_sb[:, 0], start=True, stop=False)
                nc.tensor.matmul(top_acc[m % 2][:], wt1_sb[:, 1, cols], z_sb[:, 1], start=False, stop=False)
                nc.tensor.matmul(top_acc[m % 2][:], wt1d_sb[:, cols], dense_sb[:], start=False, stop=True
                                 ).then_inc(top1_done, 1)
            for m in range(TOP2 // P):
                cols = slice(m * P, (m + 1) * P)
                for k in range(TOP1 // P):
                    pe.wait_ge(top1_ready, max(k + 1, TOP1 // P - 1 + m))
                    done = nc.tensor.matmul(top_acc[m % 2][:], wt2_sb[:, k, cols], top1_sb[:, k],
                                            start=(k == 0), stop=(k == TOP1 // P - 1))
                done.then_inc(top2_done, 1)
            for k in range(TOP2 // P):
                pe.wait_ge(top2_ready, k + 1)
                done = nc.tensor.matmul(top_acc[0][0:1], wt3_sb[:, k:k + 1], top2_sb[:, k],
                                        start=(k == 0), stop=(k == TOP2 // P - 1))
            done.then_inc(y_done, 1)


def kernel(**inputs):
    import numpy as np
    import concourse.bacc as bacc
    from concourse import mybir
    from concourse.bass_utils import run_bass_kernel_spmd as run

    def laid(a):
        return np.ascontiguousarray(a)

    a = {k: np.asarray(v) for k, v in inputs.items()}
    tables = [a[f"tbl_{f}"] for f in range(FIELDS)]
    starts = np.concatenate([[0], np.cumsum([t.shape[0] for t in tables])])[:FIELDS]

    def spread(per_row):
        padded = np.zeros((BATCH, GATHERS * LANES), np.int32)
        padded[:, :FIELDS] = per_row
        v = padded.reshape(CHUNKS, CHUNK_B, GATHERS, LANES).transpose(3, 1, 0, 2)
        return laid(v.reshape(P, CHUNKS * GATHERS))

    f = np.arange(FIELDS)
    w0 = a["L0_rec_W0"].reshape(FIELDS, FIELDS, CHANNELS)
    w0a = np.zeros((TILES0, PER_TILE, FIELDS, CHANNELS), w0.dtype)
    w0b = np.zeros_like(w0a)
    for k in range(DISTS):
        w0a[k // PER_TILE, k % PER_TILE] = w0[f, (f + k) % FIELDS]
        if k:
            w0b[k // PER_TILE, k % PER_TILE] = w0[(f + k) % FIELDS, f]
    arrays = {
        "ids": spread(a["ids"]),
        "bases": spread(np.broadcast_to(starts.astype(np.int32), (BATCH, FIELDS))),
        "table": np.concatenate(tables, axis=0),
        "w0a": laid(w0a.reshape(TILES0, ROWS0, CHANNELS).transpose(1, 0, 2)),
        "w0b": laid(w0b.reshape(TILES0, ROWS0, CHANNELS).transpose(1, 0, 2)),
        "w1": laid(a["L0_rec_W1"]),
        "w2": laid(a["L0_rec_W2"]),
        "cin_b": laid(np.stack([a["L0_rec_b0"], a["L0_rec_b1"], a["L0_rec_b2"]], axis=1)),
        "dense": laid(a["dense_ctx"].T),
        "wt1": laid(a["W_top1"]),
        "wt2": laid(a["W_top2"]),
        "wt3": laid(a["W_top3"].reshape(TOP2 // P, P).T),
        "bt1": laid(a["b_top1"].reshape(TOP1 // P, P).T),
        "bt2": laid(a["b_top2"].reshape(TOP2 // P, P).T),
    }
    nc = bacc.Bacc("TRN2", target_bir_lowering=False, num_devices=1)
    args = [nc.dram_tensor(f"in_{n}", v.shape, mybir.dt.from_np(v.dtype), kind="ExternalInput").ap()
            for n, v in arrays.items()]
    out = nc.dram_tensor("out_y", (BATCH, 1), mybir.dt.float32, kind="ExternalOutput").ap()
    build(nc, *args, out)
    r = run(nc, [{f"in_{n}": v for n, v in arrays.items()}], core_ids=[0])
    return r.results[0]["out_y"]
```

```python
import concourse.bass as bass
from concourse import mybir
from contextlib import ExitStack

BATCH, FIELDS, DIM = 512, 39, 16
CHANNELS = 128
HIDDEN = CHANNELS // 2
DENSE, TOP1, TOP2 = 16, 512, 256
P = 128

CHUNK_B = 32
COLS = CHUNK_B * DIM
CHUNKS = BATCH // CHUNK_B
CHUNKS_PADDED = CHUNKS + 1

LANES = P // CHUNK_B
GATHERS = -(-FIELDS // LANES)
LAST_LANES = FIELDS - (GATHERS - 1) * LANES

DISTS = FIELDS // 2 + 1
PER_TILE = P // FIELDS
TILES0 = -(-DISTS // PER_TILE)
ROWS0 = PER_TILE * FIELDS
LAST_ROWS0 = (DISTS - (TILES0 - 1) * PER_TILE) * FIELDS
WRAP_GATHERS = 5
WRAP = WRAP_GATHERS * LANES
ROWS_X = FIELDS + WRAP

TILES = -(-FIELDS // 2)

UNIT = 2
KINDS = {1: "SNDSNSDSNN", 0: "SDSN", 2: "NSDSNSDSNN"}


AHEAD_OF_STEP = {1: 0, 0: 1, 2: -1}


class Unit:
    def __init__(self, layer, i, kind, place):
        tiles = TILES if layer else TILES0
        self.layer, self.kind, self.place = layer, kind, place
        self.t0, self.n = UNIT * i, min(UNIT, tiles - UNIT * i)
        self.first, self.last = i == 0, UNIT * (i + 1) >= tiles
        self.rows = P if layer else ROWS0
        self.split = kind in "SD"


UNITS = []
for _layer in (1, 0, 2):
    for _i, _kind in enumerate(KINDS[_layer]):
        UNITS.append(Unit(_layer, _i, _kind, len(UNITS)))
LAYER = {layer: [u for u in UNITS if u.layer == layer] for layer in (0, 1, 2)}
PRODUCT_SLOTS, Z_SLOTS, ZP_SLOTS, HI_SLOTS, LO_SLOTS = 3, 2, 1, 4, 3
GATHERS_AFTER = [1, 1, 1, 2, 1, 1, 0, 1, 1, 1]
SUB_LAG = 2
LAG = {1: 5, 0: 5, 2: 5}
X_TO_PSUM = 2


class Ring:

    def __init__(self, kinds, slots):
        self.members = [u for u in UNITS if u.kind in kinds]
        self.per_step, self.slots = len(self.members), slots
        self.index, self.freed_by = {}, {}
        newest = {}
        n = 0
        for step in range(-1, CHUNKS + 1):
            for k, u in enumerate(self.members):
                if not 0 <= step + AHEAD_OF_STEP[u.layer] < CHUNKS:
                    continue
                self.index[step, u.place] = n
                slot = self._slot(step % 2, k)
                self.freed_by[step, u.place] = newest.get(slot, 0)
                n += 1
                newest[slot] = n

    def _slot(self, parity, k):
        return (parity * self.per_step + k) % self.slots

    def slot(self, s, u):
        return self._slot(s.u, self.members.index(u))

    def _at(self, table, step, u):
        if isinstance(step, tuple):
            c, parity = step
            first = 2 + parity
            value = table[first, u.place]
            assert all(table[s, u.place] == value + (s - first) * self.per_step
                       for s in range(first, CHUNKS - 2, 2))
            return c * self.per_step + (value - first * self.per_step)
        return table[step, u.place]

    def done(self, step, u):
        return self._at(self.index, step, u) + 1

    def free(self, step, u):
        return self._at(self.freed_by, step, u)

    def must_wait(self, s, u):
        return not s.static or self.free(s.c, u) > 0


PART = 2
FIELD_PARTS = len(LAYER[1]) // PART

WHOLE = Ring("N", PRODUCT_SLOTS)
Z = Ring("S", Z_SLOTS)
ZP = Ring("D", ZP_SLOTS)
HI = Ring("SD", HI_SLOTS)
LO = Ring("SD", LO_SLOTS)

F32 = mybir.dt.float32
F32R = mybir.dt.float32r
I32 = mybir.dt.int32
ALU = mybir.AluOpType
ACT = mybir.ActivationFunctionType
AX = mybir.AxisListType


class Step:

    def __init__(self, c, u, turn):
        self.c, self.u, self.turn = c, u, turn
        self.static = isinstance(c, int)
        self.key = c if self.static else (c, u)

    def before(self, n):
        return self.static and self.c < n

    def has(self, ahead):
        return not self.static or 0 <= self.c + ahead < CHUNKS

    def gathers(self):
        return not self.static or self.c + 3 < CHUNKS_PADDED

    def units(self, kinds="NSD"):
        return [u for u in UNITS if u.kind in kinds and self.has(AHEAD_OF_STEP[u.layer])]



def run_steps(engine, step):
    step(Step(0, 0, 0))
    step(Step(1, 1, 0))
    with engine.Fori(1, CHUNKS // 2 - 1) as i:
        step(Step(2 * i, 0, i))
        step(Step(2 * i + 1, 1, i))
    step(Step(CHUNKS - 2, 0, CHUNKS // 2 - 1))
    step(Step(CHUNKS - 1, 1, CHUNKS // 2 - 1))
    step(Step(CHUNKS, 0, CHUNKS // 2))


BEFORE = Step(-1, 1, 0)


def build(nc, ids, bases, table, w0a, w0b, w1, w2, cin_b, dense, wt1, wt2, wt3, bt1, bt2, out):
    ctx = ExitStack()
    with ctx:
        def sb(name, shape, dt=F32):
            return ctx.enter_context(nc.sbuf_tensor(name, shape, dt))

        def pb(name, shape):
            return ctx.enter_context(nc.psum_tensor(name, shape, F32))

        def sem(name):
            return ctx.enter_context(nc.semaphore(name))

        ids_sb = sb("ids_sb", [P, CHUNKS_PADDED * GATHERS], I32)
        bases_sb = sb("bases_sb", [P, CHUNKS_PADDED * GATHERS], I32)
        rows_all = sb("rows_all", [P, CHUNKS_PADDED * GATHERS], I32)
        rows_now = sb("rows_now", [P, 2, GATHERS], I32)
        looked_up = sb("looked_up", [P, 2, GATHERS, DIM])
        x_dram = nc.dram_tensor("x_scratch", (CHUNKS_PADDED * ROWS_X, COLS), F32, kind="Internal").ap()
        pair_x = sb("pair_x", [ROWS0, TILES0 + 1, COLS])
        field_x = sb("field_x", [P, 2, TILES, COLS])
        whole = sb("whole", [P, PRODUCT_SLOTS, UNIT, COLS])
        z = sb("z", [P, Z_SLOTS, UNIT, COLS])
        z_hi = sb("z_hi", [P, HI_SLOTS, UNIT, COLS], F32R)
        z_lo = sb("z_lo", [P, LO_SLOTS, UNIT, COLS], F32R)
        w_whole = sb("w_whole", [P, len(WHOLE.members), UNIT, CHANNELS])
        w_hi = sb("w_hi", [P, len(HI.members), UNIT, CHANNELS], F32R)
        w_lo = sb("w_lo", [P, len(HI.members), UNIT, CHANNELS], F32R)
        cin_b_sb = sb("cin_b_sb", [P, 3])
        direct01 = sb("direct01", [P, 2, COLS])
        direct2 = sb("direct2", [P, COLS])
        sums = sb("sums", [P, 2, BATCH])
        wt3_sb = sb("wt3_sb", [P, TOP2 // P])
        bt1_sb = sb("bt1_sb", [P, TOP1 // P])
        bt2_sb = sb("bt2_sb", [P, TOP2 // P])

        def reuse(parity, tile, rows, cols):
            n = -(-cols // COLS)
            flat = field_x[0:rows, parity, tile:tile + n].rearrange("p t c -> p (t c)")
            return flat[:, 0:cols], tile + n

        tile = 0
        staged = {}
        for layer, rows, tiles in ((1, P, TILES), (2, P, TILES), (0, ROWS0, TILES0), (3, ROWS0, TILES0)):
            v, tile = reuse(1, tile, rows, tiles * CHANNELS)
            staged[layer] = v.rearrange("p (t l) -> p t l", l=CHANNELS)
        w0b_staged = staged.pop(3)
        assert tile < TILES - 1
        v, tile = reuse(0, 0, P, 2 * TOP1)
        wt1_sb = v.rearrange("p (k n) -> p k n", n=TOP1)
        wt1d_sb, tile = reuse(0, tile, DENSE, TOP1)
        dense_sb, tile = reuse(0, tile, DENSE, BATCH)
        v, tile = reuse(0, tile, P, TOP1 // P * TOP2)
        wt2_sb = v.rearrange("p (k n) -> p k n", n=TOP2)
        v, tile = reuse(0, tile, P, TOP1 // P * BATCH)
        top1_sb = v.rearrange("p (k n) -> p k n", n=BATCH)
        v, tile = reuse(0, tile, P, TOP2 // P * BATCH)
        top2_sb = v.rearrange("p (k n) -> p k n", n=BATCH)
        y_sb, tile = reuse(0, tile, 1, BATCH)
        assert tile < TILES

        acc = [pb(f"acc{i}", [P, COLS]) for i in range(2)]
        x_psum = pb("x_psum", [P, COLS])
        hidden1 = pb("hidden1", [P, COLS])
        hidden2 = [pb(f"hidden2_{i}", [P, COLS]) for i in range(2)]
        zp = pb("zp", [P, ZP_SLOTS, UNIT, COLS])
        top1_acc = [zp[:, 0, 0], zp[:, 0, 1], hidden1[:], x_psum[:]]
        top2_acc = [acc[0][:], acc[1][:]]
        y_acc = hidden2[0][0:1]

        def acc_of(layer, s):
            if s is BEFORE:
                return acc[0]
            return acc[s.u if layer == 0 else 1 - s.u]

        pool_passed = sem("pool_passed")
        sp_passed = sem("sp_passed")
        rows_loaded = sem("rows_loaded")
        rows_added = sem("rows_added")
        rows_ready = sem("rows_ready")
        gathered = [sem("gathered0"), sem("gathered1")]
        x_stored = [sem("x_stored0"), sem("x_stored1")]
        pair_x_loaded = sem("pair_x_loaded")
        field_x_loaded = [[sem(f"field_x{u}_part{g}_loaded") for g in range(FIELD_PARTS)] for u in range(2)]
        pads_zeroed = sem("pads_zeroed")
        w_staged = [sem(f"w{layer}_staged") for layer in range(3)]
        w0_folded = sem("w0_folded")
        w_hi_ready = sem("w_hi_ready")
        w_lo_ready = sem("w_lo_ready")
        biases_loaded = sem("biases_loaded")
        top_loaded = sem("top_loaded")
        whole_ready = sem("whole_ready")
        whole_used = sem("whole_used")
        z_ready = sem("z_ready")
        z_split = sem("z_split")
        zp_ready = sem("zp_ready")
        zp_split = sem("zp_split")
        hi_ready = sem("hi_ready")
        split_used = sem("split_used")
        x_in_psum = sem("x_in_psum")
        hidden_ready = [sem("hidden1_ready"), sem("hidden2_ready")]
        drained = [sem(f"layer{layer}_drained") for layer in range(3)]
        summed01 = sem("summed01")
        summed2 = sem("summed2")
        top1_done = sem("top1_done")
        top1_ready = sem("top1_ready")
        top2_done = sem("top2_done")
        top2_ready = sem("top2_ready")
        y_done = sem("y_done")
        y_ready = sem("y_ready")
        y_stored = sem("y_stored")
        TOP_LOADS = 7

        STORE_INC = 16 * 2 * LANES
        HALVES = 2

        def before_step(s, unit):
            if s.static:
                return WHOLE.done(s.c - 1, unit)
            return WHOLE.done(s.key, unit) - WHOLE.per_step

        block = ctx.enter_context(nc.Block())

        @block.gpsimd
        def _(pool):
            pool.wait_ge(rows_loaded, 32)
            nc.gpsimd.tensor_tensor(rows_all[:], ids_sb[:], bases_sb[:], ALU.add).then_inc(rows_added, 1)
            pool.wait_ge(rows_added, 1)

            def take_rows(c, u, turn):
                if not (isinstance(c, int) and c < 2):
                    pool.wait_ge(x_stored[u], turn * STORE_INC)
                nc.gpsimd.tensor_copy(rows_now[:, u], rows_all[:, bass.ds(c * GATHERS, GATHERS)]
                                      ).then_inc(rows_ready, 1)
                pool.wait_ge(rows_ready, c + 1)

            def gather(u, j):
                n = P if j < GATHERS - 1 else LAST_LANES * CHUNK_B
                pool.indirect_dma_start(
                    looked_up[0:n, u, j], None, table,
                    bass.IndirectOffsetOnAxis(ap=rows_now[0:n, u, j:j + 1], axis=0),
                ).then_inc(gathered[u], 16)

            def low_part(s, unit):
                pool.wait_ge(hi_ready, HI.done(s.key, unit))
                if LO.must_wait(s, unit):
                    pool.wait_ge(split_used, LO.free(s.key, unit))
                at = slice(0, unit.rows)
                nc.gpsimd.tensor_tensor(
                    z_lo[at, LO.slot(s, unit), 0:unit.n], z[at, Z.slot(s, unit), 0:unit.n],
                    z_hi[at, HI.slot(s, unit), 0:unit.n].bitcast(F32), ALU.subtract).then_inc(z_split, 1)

            for c in range(3):
                take_rows(c, c % 2, c // 2)
                for j in range(GATHERS):
                    gather(c % 2, j)
            for unit in LAYER[0]:
                if unit.kind == "S":
                    low_part(BEFORE, unit)

            def step(s):
                if s.gathers():
                    take_rows(s.c + 3, 1 - s.u, s.turn + 1 + s.u)
                j = 0
                for k, unit in enumerate(s.units("S")):
                    low_part(s, unit)
                    if s.gathers():
                        for _ in range(GATHERS_AFTER[k]):
                            gather(1 - s.u, j)
                            j += 1
                while s.gathers() and j < GATHERS:
                    gather(1 - s.u, j)
                    j += 1

            run_steps(pool, step)

        @block.sync
        def _(sp):
            def wait_counted(s, semaphore, value):
                sp.wait_ge(semaphore, value)
                if not s.static:
                    sp.sem_inc(sp_passed, 1)

            def store_x(s, c, u, turn):
                wait_counted(s, gathered[u], (turn + 1) * 16 * GATHERS)
                for first_row, gathers in ((0, GATHERS), (FIELDS, WRAP_GATHERS)):
                    for lane in range(LANES):
                        n = gathers - (gathers == GATHERS and lane >= LAST_LANES)
                        dst = bass.AP(x_dram.tensor, (c * ROWS_X + first_row + lane) * COLS,
                                      [[DIM, CHUNK_B], [LANES * COLS, n], [1, DIM]])
                        sp.dma_start(dst, looked_up[lane * CHUNK_B:(lane + 1) * CHUNK_B, u, 0:n, :]
                                     ).then_inc(x_stored[u], 16)

            def load_pair_x(s, c, u, turn):
                wait_counted(s, x_stored[u], (turn + 1) * STORE_INC)
                for i in range(PER_TILE):
                    src = bass.AP(x_dram.tensor, c * ROWS_X * COLS, [[COLS, FIELDS], [1, COLS]])
                    sp.dma_start(pair_x[i * FIELDS:(i + 1) * FIELDS, TILES0], src
                                 ).then_inc(pair_x_loaded, 16)
                for i in range(PER_TILE):
                    src = bass.AP(x_dram.tensor, (c * ROWS_X + i) * COLS,
                                  [[COLS, FIELDS], [PER_TILE * COLS, TILES0], [1, COLS]])
                    sp.dma_start(pair_x[i * FIELDS:(i + 1) * FIELDS, 0:TILES0], src
                                 ).then_inc(pair_x_loaded, 16)

            def load_field_x(c, u, part):
                t0 = part * PART * UNIT
                for half in range(HALVES):
                    n = min(t0 + PART * UNIT, (FIELDS + 1 - half) // 2) - t0
                    src = bass.AP(x_dram.tensor, (c * ROWS_X + 2 * t0 + half) * COLS,
                                  [[0, HIDDEN], [2 * COLS, n], [1, COLS]])
                    sp.dma_start(field_x[half * HIDDEN:(half + 1) * HIDDEN, u, t0:t0 + n], src
                                 ).then_inc(field_x_loaded[u][part], 16)

            def load_top():
                for dst, src in ((wt1_sb, wt1[0:2 * P].rearrange("(k p) n -> p k n", p=P)),
                                 (wt1d_sb, wt1[2 * P:2 * P + DENSE]), (dense_sb, dense),
                                 (wt2_sb, wt2.rearrange("(k p) n -> p k n", p=P)),
                                 (wt3_sb[:], wt3), (bt1_sb[:], bt1), (bt2_sb[:], bt2)):
                    sp.dma_start(dst, src).then_inc(top_loaded, 16)

            store_x(BEFORE, 0, 0, 0)
            load_pair_x(BEFORE, 0, 0, 0)
            for part in range(FIELD_PARTS):
                load_field_x(0, 0, part)
            store_x(BEFORE, 1, 1, 0)
            sp.wait_ge(whole_ready, WHOLE.done(-1, LAYER[0][-1]))
            load_pair_x(BEFORE, 1, 1, 0)
            store_x(BEFORE, 2, 0, 1)

            def step(s):
                if s.has(2):
                    wait_counted(s, whole_ready, WHOLE.done(s.key, LAYER[0][-1]))
                    load_pair_x(s, s.c + 2, s.u, s.turn + 1)
                if s.before(1):
                    sp.wait_ge(w_hi_ready, 3)
                    sp.wait_ge(w_lo_ready, 3)
                for part in range(FIELD_PARTS):
                    if s.has(-1):
                        unit = LAYER[2][(part + 1) * PART - 1]
                        ring, made = {"N": (WHOLE, whole_ready), "S": (Z, z_ready),
                                      "D": (ZP, zp_ready)}[unit.kind]
                        wait_counted(s, made, ring.done(s.key, unit))
                    if s.has(1):
                        load_field_x(s.c + 1, 1 - s.u, part)
                if s.static and s.c == CHUNKS - 1:
                    load_top()
                if s.gathers():
                    store_x(s, s.c + 3, 1 - s.u, s.turn + 1 + s.u)

            run_steps(sp, step)
            assert CHUNKS_PADDED % 2 == 1
            sp.wait_ge(x_stored[0], (CHUNKS_PADDED + 1) // 2 * STORE_INC)
            sp.wait_ge(y_ready, 1)
            sp.dma_start(out.rearrange("b o -> o b"), y_sb).then_inc(y_stored, 16)
            sp.wait_ge(y_stored, 16)

        @block.scalar
        def _(act):
            act.dma_start(ids_sb[:], ids).then_inc(rows_loaded, 16)
            act.dma_start(bases_sb[:], bases).then_inc(rows_loaded, 16)
            act.dma_start(staged[0], w0a).then_inc(w_staged[0], 16)
            act.dma_start(w0b_staged, w0b).then_inc(w_staged[0], 16)
            act.dma_start(cin_b_sb[:], cin_b).then_inc(biases_loaded, 16)
            for layer, w in ((1, w1), (2, w2)):
                full = (TILES - 1) * P
                act.dma_start(staged[layer][:, 0:TILES - 1], w[0:full].rearrange("(t p) l -> p t l", p=P)
                              ).then_inc(w_staged[layer], 16)
                act.dma_start(staged[layer][0:HIDDEN, TILES - 1], w[full:full + HIDDEN]
                              ).then_inc(w_staged[layer], 16)
            act.wait_ge(biases_loaded, 16)
            act.wait_ge(pads_zeroed, 4)
            for layer in range(3):
                if layer == 0:
                    act.wait_ge(w0_folded, 1)
                else:
                    act.wait_ge(w_staged[layer], 32)
                for unit in LAYER[layer]:
                    src = staged[layer][0:unit.rows, unit.t0:unit.t0 + unit.n]
                    ring, dst = (HI, w_hi) if unit.split else (WHOLE, w_whole)
                    k = ring.members.index(unit)
                    done = nc.scalar.activation(dst[0:unit.rows, k, 0:unit.n], src, ACT.Copy)
                done.then_inc(w_hi_ready, 1)

            def relu(dst, src, bias):
                return nc.scalar.activation(dst, src, ACT.Relu, bias=bias)

            def x_to_psum(c, products_made):
                act.wait_ge(pair_x_loaded, (c + 1) * 2 * PER_TILE * 16)
                if products_made is not None:
                    act.wait_ge(whole_ready, products_made)
                nc.scalar.activation(x_psum[0:ROWS0], pair_x[:, TILES0], ACT.Copy).then_inc(x_in_psum, 1)

            def high_part(s, unit):
                if unit.split:
                    at, slot = slice(0, unit.rows), HI.slot(s, unit)
                    if HI.must_wait(s, unit):
                        act.wait_ge(split_used, HI.free(s.key, unit))
                    if unit.kind == "S":
                        act.wait_ge(z_ready, Z.done(s.key, unit))
                        src = z[at, Z.slot(s, unit), 0:unit.n]
                    else:
                        act.wait_ge(zp_ready, ZP.done(s.key, unit))
                        src = zp[at, ZP.slot(s, unit), 0:unit.n]
                    nc.scalar.activation(z_hi[at, slot, 0:unit.n], src, ACT.Copy).then_inc(hi_ready, 1)

            def to_hidden(layer, dst, src):
                lo = slice(0, HIDDEN)
                relu(dst[lo], src[lo], cin_b_sb[lo, layer:layer + 1])
                relu(dst[HIDDEN:P], src[lo], cin_b_sb[lo, layer:layer + 1]).then_inc(hidden_ready[layer], 1)

            def to_direct(layer, dst, src):
                hi = slice(HIDDEN, P)
                relu(dst, src[hi], cin_b_sb[hi, layer:layer + 1]).then_inc(drained[layer], 1)

            def finish_layer0(s, c, u):
                act.wait_ge(whole_used, WHOLE.done(s.key, LAYER[0][-1]))
                src = acc_of(0, s)
                to_hidden(0, hidden1, src)
                if not (isinstance(c, int) and c < 2):
                    act.wait_ge(summed01, c - 1)
                to_direct(0, direct01[0:HIDDEN, u], src)

            def finish_layer1(s):
                act.wait_ge(whole_used, WHOLE.done(s.key, LAYER[1][-1]))
                src = acc_of(1, s)
                to_hidden(1, hidden2[s.u], src)
                to_direct(1, direct01[HIDDEN:P, s.u], src)

            def finish_layer2(value, c, src):
                act.wait_ge(whole_used, value)
                if not (isinstance(c, int) and c < 1):
                    act.wait_ge(summed2, c)
                relu(direct2[:], src[:], cin_b_sb[:, 2:3]).then_inc(drained[2], 1)

            x_to_psum(0, None)
            for unit in LAYER[0]:
                high_part(BEFORE, unit)
            finish_layer0(BEFORE, 0, 0)

            def step(s):
                later = {}

                def at(place, what):
                    later.setdefault(place, []).append(what)

                units = s.units()
                last_place = units[-1].place
                if s.has(1):
                    at(X_TO_PSUM, lambda: x_to_psum(s.c + 1, before_step(s, LAYER[0][-1])))
                if s.has(-2):
                    at(LAG[2] - 1, lambda: finish_layer2(before_step(s, LAYER[2][-1]), s.c - 2, acc[s.u]))
                if s.has(0):
                    at(min(last_place, LAYER[1][-1].place + LAG[1]), lambda: finish_layer1(s))
                if s.has(1):
                    at(min(last_place, LAYER[0][-1].place + LAG[0]), lambda: finish_layer0(s, s.c + 1, 1 - s.u))
                for place in range(len(UNITS)):
                    for unit in units:
                        if unit.place == place:
                            high_part(s, unit)
                    for what in later.get(place, []):
                        what()

            run_steps(act, step)
            finish_layer2(WHOLE.done(CHUNKS, LAYER[2][-1]), CHUNKS - 1, acc[1])

            act.wait_ge(top_loaded, TOP_LOADS * 16)
            for m in range(TOP1 // P):
                act.wait_ge(top1_done, m + 1)
                relu(top1_sb[:, m], top1_acc[m], bt1_sb[:, m:m + 1]).then_inc(top1_ready, 1)
            for m in range(TOP2 // P):
                act.wait_ge(top2_done, m + 1)
                relu(top2_sb[:, m], top2_acc[m], bt2_sb[:, m:m + 1]).then_inc(top2_ready, 1)
            act.wait_ge(y_done, 1)
            nc.scalar.activation(y_sb, y_acc, ACT.Copy).then_inc(y_ready, 1)

        @block.vector
        def _(dve):
            upper = slice(HIDDEN, P)
            for u in range(2):
                nc.vector.memset(field_x[upper, u, TILES - 1], 0.0).then_inc(pads_zeroed, 1)
            for layer in (1, 2):
                nc.vector.memset(staged[layer][upper, TILES - 1], 0.0).then_inc(pads_zeroed, 1)
            dve.wait_ge(pads_zeroed, 4)
            dve.wait_ge(w_staged[0], 32)
            nc.vector.tensor_tensor(staged[0], staged[0], w0b_staged, ALU.add).then_inc(w0_folded, 1)
            for layer in range(3):
                dve.wait_ge(w_hi_ready, layer + 1)
                for unit in LAYER[layer]:
                    if unit.split:
                        at, k = slice(0, unit.rows), HI.members.index(unit)
                        done = nc.vector.tensor_tensor(
                            w_lo[at, k, 0:unit.n], staged[layer][at, unit.t0:unit.t0 + unit.n],
                            w_hi[at, k, 0:unit.n].bitcast(F32), ALU.subtract)
                done.then_inc(w_lo_ready, 1)

            def product(s, unit):
                at, n, tiles = slice(0, unit.rows), unit.n, slice(unit.t0, unit.t0 + unit.n)
                ring, buffer, ready, freed = {
                    "N": (WHOLE, whole, whole_ready, whole_used),
                    "S": (Z, z, z_ready, z_split),
                    "D": (ZP, zp, zp_ready, zp_split)}[unit.kind]
                dst = buffer[at, ring.slot(s, unit), 0:n]
                if ring.must_wait(s, unit):
                    dve.wait_ge(freed, ring.free(s.key, unit))
                if unit.layer == 0:
                    x, h = pair_x[:, tiles], x_psum[0:ROWS0]
                elif unit.layer == 1:
                    x, h = field_x[:, s.u, tiles], hidden1[:]
                else:
                    x, h = field_x[:, 1 - s.u, tiles], hidden2[1 - s.u][:]
                h = h.unsqueeze(1).to_broadcast([unit.rows, n, COLS])
                nc.vector.tensor_tensor(dst, x, h, ALU.mult).then_inc(ready, 1)

            def low_part(s, unit):
                dve.wait_ge(hi_ready, HI.done(s.key, unit))
                if LO.must_wait(s, unit):
                    dve.wait_ge(split_used, LO.free(s.key, unit))
                at = slice(0, unit.rows)
                nc.vector.tensor_tensor(
                    z_lo[at, LO.slot(s, unit), 0:unit.n], zp[at, ZP.slot(s, unit), 0:unit.n],
                    z_hi[at, HI.slot(s, unit), 0:unit.n].bitcast(F32), ALU.subtract).then_inc(zp_split, 1)

            def sum_components(k, c, src, done, value, summed):
                dve.wait_ge(done, value)
                nc.vector.tensor_reduce(
                    out=sums[:, k, bass.ds(c * CHUNK_B, CHUNK_B)],
                    in_=src.rearrange("p (b d) -> p b d", d=DIM),
                    axis=AX.X, op=ALU.add).then_inc(summed, 1)

            def products(s, units):
                waiting = []
                for unit in units:
                    if unit.first and unit.layer == 0:
                        dve.wait_ge(x_in_psum, s.c + 2)
                    if unit.first and unit.layer == 1:
                        dve.wait_ge(hidden_ready[0], s.c + 1)
                    if unit.first and unit.layer == 2:
                        dve.wait_ge(hidden_ready[1], s.c)
                    part, within = divmod(unit.t0 // UNIT, PART)
                    if unit.layer == 1 and within == 0:
                        dve.wait_ge(field_x_loaded[s.u][part], (s.turn + 1) * HALVES * 16)
                    if unit.kind == "D":
                        assert not waiting, "zp has one slot"
                    product(s, unit)
                    if unit.kind == "D":
                        waiting.append(unit)
                    if waiting and (waiting[0].place <= unit.place - SUB_LAG or unit is units[-1]):
                        low_part(s, waiting.pop(0))
                    if unit.place == LAG[2] + 1 and s.has(-2):
                        sum_components(1, s.c - 2, direct2[:], drained[2], s.c - 1, summed2)
                    if unit.place == LAYER[1][-1].place + LAG[1] + 1 and s.has(0):
                        sum_components(0, s.c, direct01[:, s.u], drained[1], s.c + 1, summed01)

            products(BEFORE, LAYER[0])

            def step(s):
                products(s, s.units())
                if s.static and s.c == 0:
                    sum_components(0, 0, direct01[:, 0], drained[1], 1, summed01)
                if s.static and s.c == CHUNKS:
                    sum_components(1, CHUNKS - 2, direct2[:], drained[2], CHUNKS - 1, summed2)

            run_steps(dve, step)
            sum_components(1, CHUNKS - 1, direct2[:], drained[2], CHUNKS, summed2)

        @block.tensor
        def _(pe):
            def contract(s, unit):
                at = slice(0, unit.rows)
                dst = acc_of(unit.layer, s)[:]

                def passes(w, v, tiles, start, stop):
                    for k in tiles:
                        done = nc.tensor.matmul(dst, w[at, k], v[at, k], start=start and k == 0,
                                                stop=stop and k == unit.n - 1)
                    return done

                if unit.kind == "N":
                    pe.wait_ge(whole_ready, WHOLE.done(s.key, unit))
                    w = w_whole[:, WHOLE.members.index(unit)]
                    passes(w, whole[:, WHOLE.slot(s, unit)], range(unit.n), unit.first, unit.last
                           ).then_inc(whole_used, 1)
                    return
                k, hi, lo = HI.members.index(unit), HI.slot(s, unit), LO.slot(s, unit)
                pe.wait_ge(hi_ready, HI.done(s.key, unit))
                passes(w_hi[:, k], z_hi[:, hi], range(unit.n), unit.first, False)
                passes(w_lo[:, k], z_hi[:, hi], range(unit.n), False, False)
                if unit.kind == "S":
                    pe.wait_ge(z_split, Z.done(s.key, unit))
                else:
                    pe.wait_ge(zp_split, ZP.done(s.key, unit))
                passes(w_hi[:, k], z_lo[:, lo], range(unit.n), False, False).then_inc(split_used, 1)

            pe.wait_ge(w_lo_ready, 1)
            for unit in LAYER[0]:
                contract(BEFORE, unit)
            pe.wait_ge(w_lo_ready, 3)

            def step(s):
                for unit in s.units():
                    if unit.first:
                        if unit.layer == 1:
                            pe.wait_ge(drained[0], s.c + 1)
                        elif unit.layer == 2:
                            pe.wait_ge(drained[1], s.c + 1 if s.has(0) else s.c)
                        elif s.has(-2):
                            pe.wait_ge(drained[2], s.c - 1)
                    contract(s, unit)

            run_steps(pe, step)

            pe.wait_ge(top_loaded, TOP_LOADS * 16)
            pe.wait_ge(summed01, CHUNKS)
            pe.wait_ge(whole_ready, WHOLE.done(CHUNKS, LAYER[2][-1]))
            for m in range(TOP1 // P):
                cols = slice(m * P, (m + 1) * P)
                nc.tensor.matmul(top1_acc[m], wt1_sb[:, 0, cols], sums[:, 0], start=True, stop=False)
                nc.tensor.matmul(top1_acc[m], wt1d_sb[:, cols], dense_sb, start=False, stop=False)
            pe.wait_ge(summed2, CHUNKS)
            for m in range(TOP1 // P):
                cols = slice(m * P, (m + 1) * P)
                nc.tensor.matmul(top1_acc[m], wt1_sb[:, 1, cols], sums[:, 1], start=False, stop=True
                                 ).then_inc(top1_done, 1)
            for m in range(TOP2 // P):
                cols = slice(m * P, (m + 1) * P)
                for k in range(TOP1 // P):
                    pe.wait_ge(top1_ready, k + 1)
                    done = nc.tensor.matmul(top2_acc[m], wt2_sb[:, k, cols], top1_sb[:, k],
                                            start=(k == 0), stop=(k == TOP1 // P - 1))
                done.then_inc(top2_done, 1)
            for k in range(TOP2 // P):
                pe.wait_ge(top2_ready, k + 1)
                done = nc.tensor.matmul(y_acc, wt3_sb[:, k:k + 1], top2_sb[:, k],
                                        start=(k == 0), stop=(k == TOP2 // P - 1))
            done.then_inc(y_done, 1)


def kernel(**inputs):
    import numpy as np
    import concourse.bacc as bacc
    from concourse import mybir
    from concourse.bass_utils import run_bass_kernel_spmd as run

    def laid(a):
        return np.ascontiguousarray(a)

    a = {k: np.asarray(v) for k, v in inputs.items()}
    tables = [a[f"tbl_{f}"] for f in range(FIELDS)]
    starts = np.concatenate([[0], np.cumsum([t.shape[0] for t in tables])])[:FIELDS]

    def spread(per_row):
        padded = np.zeros((CHUNKS_PADDED * CHUNK_B, GATHERS * LANES), np.int32)
        padded[:BATCH, :FIELDS] = per_row
        v = padded.reshape(CHUNKS_PADDED, CHUNK_B, GATHERS, LANES).transpose(3, 1, 0, 2)
        return laid(v.reshape(P, CHUNKS_PADDED * GATHERS))

    f = np.arange(FIELDS)
    w0 = a["L0_rec_W0"].reshape(FIELDS, FIELDS, CHANNELS)
    w0a = np.zeros((TILES0, PER_TILE, FIELDS, CHANNELS), w0.dtype)
    w0b = np.zeros_like(w0a)
    for k in range(DISTS):
        w0a[k // PER_TILE, k % PER_TILE] = w0[f, (f + k) % FIELDS]
        if k:
            w0b[k // PER_TILE, k % PER_TILE] = w0[(f + k) % FIELDS, f]
    arrays = {
        "ids": spread(a["ids"]),
        "bases": spread(np.broadcast_to(starts.astype(np.int32), (BATCH, FIELDS))),
        "table": np.concatenate(tables, axis=0),
        "w0a": laid(w0a.reshape(TILES0, ROWS0, CHANNELS).transpose(1, 0, 2)),
        "w0b": laid(w0b.reshape(TILES0, ROWS0, CHANNELS).transpose(1, 0, 2)),
        "w1": laid(a["L0_rec_W1"]),
        "w2": laid(a["L0_rec_W2"]),
        "cin_b": laid(np.stack([a["L0_rec_b0"], a["L0_rec_b1"], a["L0_rec_b2"]], axis=1)),
        "dense": laid(a["dense_ctx"].T),
        "wt1": laid(a["W_top1"]),
        "wt2": laid(a["W_top2"]),
        "wt3": laid(a["W_top3"].reshape(TOP2 // P, P).T),
        "bt1": laid(a["b_top1"].reshape(TOP1 // P, P).T),
        "bt2": laid(a["b_top2"].reshape(TOP2 // P, P).T),
    }
    nc = bacc.Bacc("TRN2", target_bir_lowering=False, num_devices=1)
    args = [nc.dram_tensor(f"in_{n}", v.shape, mybir.dt.from_np(v.dtype), kind="ExternalInput").ap()
            for n, v in arrays.items()]
    out = nc.dram_tensor("out_y", (BATCH, 1), mybir.dt.float32, kind="ExternalOutput").ap()
    build(nc, *args, out)
    r = run(nc, [{f"in_{n}": v for n, v in arrays.items()}], core_ids=[0])
    return r.results[0]["out_y"]
```

```python
import concourse.bass as bass
from concourse import mybir
from contextlib import ExitStack

BATCH, FIELDS, DIM = 512, 39, 16
CHANNELS = 128
HIDDEN = CHANNELS // 2
DENSE, TOP1, TOP2 = 16, 512, 256
P = 128

CHUNK_B = 32
COLS = CHUNK_B * DIM
CHUNKS = BATCH // CHUNK_B

LANES = P // CHUNK_B
GATHERS = -(-FIELDS // LANES)
LAST_LANES = FIELDS - (GATHERS - 1) * LANES

DISTS = FIELDS // 2 + 1
PER_TILE = P // FIELDS
TILES0 = -(-DISTS // PER_TILE)
ROWS0 = PER_TILE * FIELDS
WRAP_GATHERS = 5
WRAP = WRAP_GATHERS * LANES
ROWS_X = FIELDS + WRAP

TILES = -(-FIELDS // 2)

UNIT = 2
KINDS = {1: "SNDSNSDSNN", 0: "SDSN", 2: "NSDSNSDSNN"}
AHEAD_OF_STEP = {1: 0, 0: 1, 2: -1}


class Unit:

    def __init__(self, layer, i, kind, place):
        tiles = TILES if layer else TILES0
        self.layer, self.kind, self.place = layer, kind, place
        self.t0, self.n = UNIT * i, min(UNIT, tiles - UNIT * i)
        self.first, self.last = i == 0, UNIT * (i + 1) >= tiles
        self.rows = P if layer else ROWS0
        self.split = kind in "SD"


UNITS = []
for _layer in (1, 0, 2):
    for _i, _kind in enumerate(KINDS[_layer]):
        UNITS.append(Unit(_layer, _i, _kind, len(UNITS)))
LAYER = {layer: [u for u in UNITS if u.layer == layer] for layer in (0, 1, 2)}


def in_order(step, kinds):
    units = LAYER[0] + LAYER[1] if step == 0 else UNITS
    return [u for u in units if u.kind in kinds]


WHOLE_SLOTS, Z_SLOTS, ZP_SLOTS, HI_SLOTS, LO_SLOTS = 3, 4, 1, 3, 3
GATHERS_AFTER = [2, 1, 1, 1, 1, 1, 1, 1, 1, 0]
SUB_LAG = 2
LAG = {1: 5, 0: 5, 2: 5}
EARLY_GATHERS = [0, 3]
FIRST_GATHERS = [1] * 6
FINISH_FIRST = 1
X_TO_PSUM = 8


class Ring:

    def __init__(self, kinds, slots):
        self.members = [u for u in UNITS if u.kind in kinds]
        self.per_step, self.slots = len(self.members), {}
        self.index, self.freed_by = {}, {}
        newest = {}
        n = 0
        assert 2 * self.per_step % slots == 0
        for step in range(-1, CHUNKS + 1):
            for u in in_order(step, kinds):
                if not 0 <= step + AHEAD_OF_STEP[u.layer] < CHUNKS:
                    continue
                self.index[step, u.place] = n
                if 1 <= step < CHUNKS - 2:
                    slot = (step % 2 * self.per_step + self.members.index(u)) % slots
                else:
                    slot = min(range(slots), key=lambda i: newest.get(i, 0))
                self.slots[step, u.place] = slot
                self.freed_by[step, u.place] = newest.get(slot, 0)
                n += 1
                newest[slot] = n

    def slot(self, s, u):
        return self.slots[s.c if s.static else 2 + s.u, u.place]

    def _at(self, table, step, u):
        if isinstance(step, tuple):
            c, parity = step
            first = 2 + parity
            value = table[first, u.place]
            assert all(table[s, u.place] == value + (s - first) * self.per_step
                       for s in range(first, CHUNKS - 2, 2))
            return c * self.per_step + (value - first * self.per_step)
        return table[step, u.place]

    def done(self, step, u):
        return self._at(self.index, step, u) + 1

    def free(self, step, u):
        return self._at(self.freed_by, step, u)

    def must_wait(self, s, u):
        return not s.static or self.free(s.c, u) > 0


PART = 2
FIELD_PARTS = len(LAYER[1]) // PART

WHOLE = Ring("N", WHOLE_SLOTS)
Z = Ring("S", Z_SLOTS)
ZP = Ring("D", ZP_SLOTS)
HI = Ring("SD", HI_SLOTS)
LO = Ring("SD", LO_SLOTS)

F32 = mybir.dt.float32
F32R = mybir.dt.float32r
I32 = mybir.dt.int32
ALU = mybir.AluOpType
ACT = mybir.ActivationFunctionType
AX = mybir.AxisListType


class Step:

    def __init__(self, c, u, turn):
        self.c, self.u, self.turn = c, u, turn
        self.static = isinstance(c, int)
        self.key = c if self.static else (c, u)

    def has(self, ahead):
        return not self.static or 0 <= self.c + ahead < CHUNKS

    def behind(self, unit, lag):
        units = self.units()
        return min(units.index(unit) + lag, len(units) - 1)

    def units(self, kinds="NSD"):
        return [u for u in in_order(self.c if self.static else None, kinds)
                if self.has(AHEAD_OF_STEP[u.layer])]


def run_steps(engine, step):
    step(Step(0, 0, 0))
    step(Step(1, 1, 0))
    with engine.Fori(1, CHUNKS // 2 - 1) as i:
        step(Step(2 * i, 0, i))
        step(Step(2 * i + 1, 1, i))
    step(Step(CHUNKS - 2, 0, CHUNKS // 2 - 1))
    step(Step(CHUNKS - 1, 1, CHUNKS // 2 - 1))
    step(Step(CHUNKS, 0, CHUNKS // 2))


BEFORE = Step(-1, 1, 0)


def build(nc, ids, bases, table, w0a, w0b, w1, w2, cin_b, dense, wt1, wt2, wt3, bt1, bt2, out):
    ctx = ExitStack()
    with ctx:
        def sb(name, shape, dt=F32):
            return ctx.enter_context(nc.sbuf_tensor(name, shape, dt))

        def pb(name, shape):
            return ctx.enter_context(nc.psum_tensor(name, shape, F32))

        def sem(name):
            return ctx.enter_context(nc.semaphore(name))

        ids_sb = sb("ids_sb", [P, CHUNKS * GATHERS], I32)
        bases_sb = sb("bases_sb", [P, CHUNKS * GATHERS], I32)
        rows_all = sb("rows_all", [P, CHUNKS * GATHERS], I32)
        rows_now = sb("rows_now", [P, 2, GATHERS], I32)
        looked_up = sb("looked_up", [P, 2, GATHERS, DIM])
        x_dram = nc.dram_tensor("x_scratch", (CHUNKS * ROWS_X, COLS), F32, kind="Internal").ap()
        pair_x = sb("pair_x", [ROWS0, TILES0 + 1, COLS])
        field_x = sb("field_x", [P, 2, TILES, COLS])
        whole = sb("whole", [P, WHOLE_SLOTS, UNIT, COLS])
        z = sb("z", [P, Z_SLOTS, UNIT, COLS])
        z_hi = sb("z_hi", [P, HI_SLOTS, UNIT, COLS], F32R)
        z_lo = sb("z_lo", [P, LO_SLOTS, UNIT, COLS], F32R)
        w_whole = sb("w_whole", [P, len(WHOLE.members), UNIT, CHANNELS])
        w_hi = sb("w_hi", [P, len(HI.members), UNIT, CHANNELS], F32R)
        w_lo = sb("w_lo", [P, len(HI.members), UNIT, CHANNELS], F32R)
        cin_b_sb = sb("cin_b_sb", [P, 3])
        direct01 = sb("direct01", [P, 2, COLS])
        direct2 = sb("direct2", [P, COLS])
        sums = sb("sums", [P, 2, BATCH])
        wt3_sb = sb("wt3_sb", [P, TOP2 // P])
        bt1_sb = sb("bt1_sb", [P, TOP1 // P])
        bt2_sb = sb("bt2_sb", [P, TOP2 // P])

        def reuse(parity, tile, rows, cols):
            n = -(-cols // COLS)
            flat = field_x[0:rows, parity, tile:tile + n].rearrange("p t c -> p (t c)")
            return flat[:, 0:cols], tile + n

        tile = 0
        staged = {}
        for layer, rows, tiles in ((1, P, TILES), (2, P, TILES), (0, ROWS0, TILES0), (3, ROWS0, TILES0)):
            v, tile = reuse(1, tile, rows, tiles * CHANNELS)
            staged[layer] = v.rearrange("p (t l) -> p t l", l=CHANNELS)
        w0b_staged = staged.pop(3)
        assert tile < TILES - 1
        v, tile = reuse(0, 0, P, 2 * TOP1)
        wt1_sb = v.rearrange("p (k n) -> p k n", n=TOP1)
        wt1d_sb, tile = reuse(0, tile, DENSE, TOP1)
        dense_sb, tile = reuse(0, tile, DENSE, BATCH)
        v, tile = reuse(0, tile, P, TOP1 // P * TOP2)
        wt2_sb = v.rearrange("p (k n) -> p k n", n=TOP2)
        v, tile = reuse(0, tile, P, TOP1 // P * BATCH)
        top1_sb = v.rearrange("p (k n) -> p k n", n=BATCH)
        v, tile = reuse(0, tile, P, TOP2 // P * BATCH)
        top2_sb = v.rearrange("p (k n) -> p k n", n=BATCH)
        y_sb, tile = reuse(0, tile, 1, BATCH)
        assert tile < TILES

        acc = [pb(f"acc{i}", [P, COLS]) for i in range(2)]
        x_psum = pb("x_psum", [P, COLS])
        hidden1 = pb("hidden1", [P, COLS])
        hidden2 = [pb(f"hidden2_{i}", [P, COLS]) for i in range(2)]
        zp = pb("zp", [P, ZP_SLOTS, UNIT, COLS])
        top1_acc = [zp[:, 0, 0], zp[:, 0, 1], hidden1[:], x_psum[:]]
        top2_acc = [acc[0][:], acc[1][:]]
        y_acc = hidden2[0][0:1]

        def acc_of(layer, s):
            if s is BEFORE:
                return acc[1]
            if s.static and s.c >= CHUNKS - 1 and layer == 2:
                return acc[s.u]
            return acc[s.u if layer == 0 else 1 - s.u]

        sp_passed = sem("sp_passed")
        rows_loaded = sem("rows_loaded")
        rows_added = sem("rows_added")
        rows_ready = sem("rows_ready")
        gathered_early = [sem("gathered_early0"), sem("gathered_early1")]
        gathered_late = [sem("gathered_late0"), sem("gathered_late1")]
        x_stored = [sem("x_stored0"), sem("x_stored1")]
        x_f_loaded = sem("x_f_loaded")
        pair_x_loaded = [sem("pair_x_part0_loaded"), sem("pair_x_part1_loaded")]
        field_x_loaded = [[sem(f"field_x{u}_part{g}_loaded") for g in range(FIELD_PARTS)] for u in range(2)]
        pads_zeroed = sem("pads_zeroed")
        w_staged = [sem(f"w{layer}_staged") for layer in range(3)]
        w0_folded = sem("w0_folded")
        w_hi_ready = sem("w_hi_ready")
        w_lo_ready = sem("w_lo_ready")
        biases_loaded = sem("biases_loaded")
        top_loaded = sem("top_loaded")
        whole_ready = sem("whole_ready")
        whole_used = sem("whole_used")
        z_ready = sem("z_ready")
        z_split = sem("z_split")
        zp_ready = sem("zp_ready")
        zp_split = sem("zp_split")
        hi_ready = sem("hi_ready")
        split_used = sem("split_used")
        x_in_psum = sem("x_in_psum")
        hidden_ready = [sem("hidden1_ready"), sem("hidden2_ready")]
        drained = [sem(f"layer{layer}_drained") for layer in range(3)]
        summed01 = sem("summed01")
        summed2 = sem("summed2")
        top1_done = sem("top1_done")
        top1_ready = sem("top1_ready")
        top2_done = sem("top2_done")
        top2_ready = sem("top2_ready")
        y_done = sem("y_done")
        y_ready = sem("y_ready")
        y_stored = sem("y_stored")
        TOP_LOADS = 7

        STORE_INC = 4 * 16
        PAIR_X_INC = PER_TILE * 16
        HALVES = 2

        def made(s, unit):
            ring, ready = {"N": (WHOLE, whole_ready), "S": (Z, z_ready), "D": (ZP, zp_ready)}[unit.kind]
            return ready, ring.done(s.key, unit)

        def before_step(s, unit):
            if s.static:
                return WHOLE.done(s.c - 1, unit)
            return WHOLE.done(s.key, unit) - WHOLE.per_step

        block = ctx.enter_context(nc.Block())

        @block.gpsimd
        def _(pool):
            pool.wait_ge(rows_loaded, 32)
            nc.gpsimd.tensor_tensor(rows_all[:], ids_sb[:], bases_sb[:], ALU.add).then_inc(rows_added, 1)
            pool.wait_ge(rows_added, 1)

            def take_rows(c, u, turn):
                if not (isinstance(c, int) and c < 2):
                    pool.wait_ge(x_stored[u], turn * STORE_INC)
                nc.gpsimd.tensor_copy(rows_now[:, u], rows_all[:, bass.ds(c * GATHERS, GATHERS)]
                                      ).then_inc(rows_ready, 1)
                pool.wait_ge(rows_ready, c + 1)

            def gather(u, j):
                n = P if j < GATHERS - 1 else LAST_LANES * CHUNK_B
                pool.indirect_dma_start(
                    looked_up[0:n, u, j], None, table,
                    bass.IndirectOffsetOnAxis(ap=rows_now[0:n, u, j:j + 1], axis=0),
                ).then_inc((gathered_early if j < WRAP_GATHERS else gathered_late)[u], 16)

            def low_part(s, unit):
                pool.wait_ge(hi_ready, HI.done(s.key, unit))
                if LO.must_wait(s, unit):
                    pool.wait_ge(split_used, LO.free(s.key, unit))
                at = slice(0, unit.rows)
                nc.gpsimd.tensor_tensor(
                    z_lo[at, LO.slot(s, unit), 0:unit.n], z[at, Z.slot(s, unit), 0:unit.n],
                    z_hi[at, HI.slot(s, unit), 0:unit.n].bitcast(F32), ALU.subtract).then_inc(z_split, 1)

            for c in range(2):
                take_rows(c, c, 0)
                for j in range(GATHERS):
                    gather(c, j)
            take_rows(2, 0, 1)
            j = 0
            for k, unit in enumerate(BEFORE.units("S")):
                low_part(BEFORE, unit)
                for _ in range(EARLY_GATHERS[k]):
                    gather(0, j)
                    j += 1

            def step(s):
                begun = s.static and s.c == 0
                if s.has(2) and not begun:
                    take_rows(s.c + 2, s.u, s.turn + 1)
                j = sum(EARLY_GATHERS) if begun else 0
                for k, unit in enumerate(s.units("S")):
                    low_part(s, unit)
                    if s.has(2):
                        for _ in range(min((FIRST_GATHERS if begun else GATHERS_AFTER)[k], GATHERS - j)):
                            gather(s.u, j)
                            j += 1
                while s.has(2) and j < GATHERS:
                    gather(s.u, j)
                    j += 1

            run_steps(pool, step)

        @block.sync
        def _(sp):
            def wait_counted(s, semaphore, value):
                sp.wait_ge(semaphore, value)
                if not s.static:
                    sp.sem_inc(sp_passed, 1)

            def store_x(s, c, u, turn):
                def store(first_row, j0, j1, lanes):
                    n = lanes * CHUNK_B
                    dst = bass.AP(x_dram.tensor, (c * ROWS_X + first_row) * COLS,
                                  [[DIM, n], [LANES * COLS, j1 - j0], [1, DIM]])
                    sp.dma_start(dst, looked_up[0:n, u, j0:j1, :]).then_inc(x_stored[u], 16)

                wait_counted(s, gathered_early[u], (turn + 1) * 16 * WRAP_GATHERS)
                store(0, 0, WRAP_GATHERS, LANES)
                store(FIELDS, 0, WRAP_GATHERS, LANES)
                wait_counted(s, gathered_late[u], (turn + 1) * 16 * (GATHERS - WRAP_GATHERS))
                store(WRAP, WRAP_GATHERS, GATHERS - 1, LANES)
                store((GATHERS - 1) * LANES, GATHERS - 1, GATHERS, LAST_LANES)

            def load_pair_x(c, part):
                t0, t1 = ((0, UNIT), (UNIT, TILES0))[part]
                groups = [slice(i * FIELDS, (i + 1) * FIELDS) for i in range(PER_TILE)]
                if part == 0:
                    for at in groups:
                        src = bass.AP(x_dram.tensor, c * ROWS_X * COLS, [[COLS, FIELDS], [1, COLS]])
                        sp.dma_start(pair_x[at, TILES0], src).then_inc(x_f_loaded, 16)
                for i, at in enumerate(groups):
                    src = bass.AP(x_dram.tensor, (c * ROWS_X + PER_TILE * t0 + i) * COLS,
                                  [[COLS, FIELDS], [PER_TILE * COLS, t1 - t0], [1, COLS]])
                    sp.dma_start(pair_x[at, t0:t1], src).then_inc(pair_x_loaded[part], 16)

            def load_field_x(c, u, part):
                t0 = part * PART * UNIT
                for half in range(HALVES):
                    n = min(t0 + PART * UNIT, (FIELDS + 1 - half) // 2) - t0
                    src = bass.AP(x_dram.tensor, (c * ROWS_X + 2 * t0 + half) * COLS,
                                  [[0, HIDDEN], [2 * COLS, n], [1, COLS]])
                    sp.dma_start(field_x[half * HIDDEN:(half + 1) * HIDDEN, u, t0:t0 + n], src
                                 ).then_inc(field_x_loaded[u][part], 16)

            def load_top():
                for dst, src in ((wt1_sb, wt1[0:2 * P].rearrange("(k p) n -> p k n", p=P)),
                                 (wt1d_sb, wt1[2 * P:2 * P + DENSE]), (dense_sb, dense),
                                 (wt2_sb, wt2.rearrange("(k p) n -> p k n", p=P)),
                                 (wt3_sb[:], wt3), (bt1_sb[:], bt1), (bt2_sb[:], bt2)):
                    sp.dma_start(dst, src).then_inc(top_loaded, 16)

            store_x(BEFORE, 0, 0, 0)
            sp.wait_ge(x_stored[0], STORE_INC)
            for part in range(2):
                load_pair_x(0, part)
            store_x(BEFORE, 1, 1, 0)
            sp.wait_ge(x_stored[1], STORE_INC)
            sp.wait_ge(x_in_psum, 1)
            sp.wait_ge(*made(BEFORE, LAYER[0][0]))
            load_pair_x(1, 0)
            sp.wait_ge(*made(BEFORE, LAYER[0][-1]))
            load_pair_x(1, 1)
            for part in range(FIELD_PARTS):
                load_field_x(0, 0, part)
            sp.wait_ge(w_hi_ready, 3)
            sp.wait_ge(w_lo_ready, 3)
            for part in range(FIELD_PARTS):
                load_field_x(1, 1, part)

            def step(s):
                for part in range(FIELD_PARTS):
                    if s.has(-1):
                        wait_counted(s, *made(s, LAYER[2][(part + 1) * PART - 1]))
                        if s.has(1):
                            load_field_x(s.c + 1, 1 - s.u, part)
                if s.static and s.c == CHUNKS - 1:
                    load_top()
                if s.has(2):
                    store_x(s, s.c + 2, s.u, s.turn + 1)
                    wait_counted(s, x_stored[s.u], (s.turn + 2) * STORE_INC)
                    wait_counted(s, *made(s, LAYER[0][-1]))
                    for part in range(2):
                        load_pair_x(s.c + 2, part)

            run_steps(sp, step)
            for u in range(2):
                sp.wait_ge(x_stored[u], CHUNKS // 2 * STORE_INC)
            sp.wait_ge(y_ready, 1)
            sp.dma_start(out.rearrange("b o -> o b"), y_sb).then_inc(y_stored, 16)
            sp.wait_ge(y_stored, 16)

        @block.scalar
        def _(act):
            act.dma_start(ids_sb[:], ids).then_inc(rows_loaded, 16)
            act.dma_start(bases_sb[:], bases).then_inc(rows_loaded, 16)
            act.dma_start(staged[0], w0a).then_inc(w_staged[0], 16)
            act.dma_start(w0b_staged, w0b).then_inc(w_staged[0], 16)
            act.dma_start(cin_b_sb[:], cin_b).then_inc(biases_loaded, 16)
            for layer, w in ((1, w1), (2, w2)):
                full = (TILES - 1) * P
                act.dma_start(staged[layer][:, 0:TILES - 1], w[0:full].rearrange("(t p) l -> p t l", p=P)
                              ).then_inc(w_staged[layer], 16)
                act.dma_start(staged[layer][0:HIDDEN, TILES - 1], w[full:full + HIDDEN]
                              ).then_inc(w_staged[layer], 16)
            act.wait_ge(biases_loaded, 16)
            act.wait_ge(pads_zeroed, 4)
            for layer in range(3):
                if layer == 0:
                    act.wait_ge(w0_folded, 1)
                else:
                    act.wait_ge(w_staged[layer], 32)
                for unit in LAYER[layer]:
                    src = staged[layer][0:unit.rows, unit.t0:unit.t0 + unit.n]
                    ring, dst = (HI, w_hi) if unit.split else (WHOLE, w_whole)
                    k = ring.members.index(unit)
                    done = nc.scalar.activation(dst[0:unit.rows, k, 0:unit.n], src, ACT.Copy)
                done.then_inc(w_hi_ready, 1)

            def relu(dst, src, bias):
                return nc.scalar.activation(dst, src, ACT.Relu, bias=bias)

            def x_to_psum(c, products_made):
                act.wait_ge(x_f_loaded, (c + 1) * PAIR_X_INC)
                if products_made is not None:
                    act.wait_ge(whole_ready, products_made)
                nc.scalar.activation(x_psum[0:ROWS0], pair_x[:, TILES0], ACT.Copy).then_inc(x_in_psum, 1)

            def high_part(s, unit):
                if unit.split:
                    at, slot = slice(0, unit.rows), HI.slot(s, unit)
                    if HI.must_wait(s, unit):
                        act.wait_ge(split_used, HI.free(s.key, unit))
                    if unit.kind == "S":
                        act.wait_ge(z_ready, Z.done(s.key, unit))
                        src = z[at, Z.slot(s, unit), 0:unit.n]
                    else:
                        act.wait_ge(zp_ready, ZP.done(s.key, unit))
                        src = zp[at, ZP.slot(s, unit), 0:unit.n]
                    nc.scalar.activation(z_hi[at, slot, 0:unit.n], src, ACT.Copy).then_inc(hi_ready, 1)

            def to_hidden(layer, dst, src):
                lo = slice(0, HIDDEN)
                relu(dst[lo], src[lo], cin_b_sb[lo, layer:layer + 1])
                relu(dst[HIDDEN:P], src[lo], cin_b_sb[lo, layer:layer + 1]).then_inc(hidden_ready[layer], 1)

            def to_direct(layer, dst, src):
                hi = slice(HIDDEN, P)
                relu(dst, src[hi], cin_b_sb[hi, layer:layer + 1]).then_inc(drained[layer], 1)

            def finish_layer0(s, c, u):
                act.wait_ge(whole_used, WHOLE.done(s.key, LAYER[0][-1]))
                if s.static and s.c == 0:
                    act.wait_ge(whole_ready, WHOLE.done(0, LAYER[1][-1]))
                src = acc_of(0, s)
                to_hidden(0, hidden1, src)
                if not (isinstance(c, int) and c < 2):
                    act.wait_ge(summed01, c - 1)
                to_direct(0, direct01[0:HIDDEN, u], src)

            def finish_layer1(s):
                act.wait_ge(whole_used, WHOLE.done(s.key, LAYER[1][-1]))
                src = acc_of(1, s)
                to_hidden(1, hidden2[s.u], src)
                to_direct(1, direct01[HIDDEN:P, s.u], src)

            def finish_layer2(value, c, src):
                act.wait_ge(whole_used, value)
                if not (isinstance(c, int) and c < 1):
                    act.wait_ge(summed2, c)
                relu(direct2[:], src[:], cin_b_sb[:, 2:3]).then_inc(drained[2], 1)

            x_to_psum(0, None)
            for unit in LAYER[0]:
                high_part(BEFORE, unit)
            x_to_psum(1, WHOLE.done(-1, LAYER[0][-1]))
            step0 = Step(0, 0, 0)
            for i, unit in enumerate(step0.units()):
                high_part(step0, unit)
                if i == FINISH_FIRST:
                    finish_layer0(BEFORE, 0, 0)
            finish_layer0(step0, 1, 1)

            def step(s):
                if s.static and s.c == 0:
                    return
                for i, unit in enumerate(s.units()):
                    high_part(s, unit)
                    if i == X_TO_PSUM and s.has(1):
                        x_to_psum(s.c + 1, before_step(s, LAYER[0][-1]))
                    if i == LAG[1] - 1 and s.static and s.c == 1:
                        finish_layer1(step0)
                    if i == LAG[2] - 1 and s.has(-2):
                        src = acc[1 if s.static and s.c == CHUNKS else s.u]
                        finish_layer2(before_step(s, LAYER[2][-1]), s.c - 2, src)
                    if s.has(0) and i == s.behind(LAYER[1][-1], LAG[1]):
                        finish_layer1(s)
                    if s.has(1) and i == s.behind(LAYER[0][-1], LAG[0]):
                        finish_layer0(s, s.c + 1, 1 - s.u)

            run_steps(act, step)
            finish_layer2(WHOLE.done(CHUNKS, LAYER[2][-1]), CHUNKS - 1, acc[0])

            act.wait_ge(top_loaded, TOP_LOADS * 16)
            for m in range(TOP1 // P):
                act.wait_ge(top1_done, m + 1)
                relu(top1_sb[:, m], top1_acc[m], bt1_sb[:, m:m + 1]).then_inc(top1_ready, 1)
            for m in range(TOP2 // P):
                act.wait_ge(top2_done, m + 1)
                relu(top2_sb[:, m], top2_acc[m], bt2_sb[:, m:m + 1]).then_inc(top2_ready, 1)
            act.wait_ge(y_done, 1)
            nc.scalar.activation(y_sb, y_acc, ACT.Copy).then_inc(y_ready, 1)

        @block.vector
        def _(dve):
            upper = slice(HIDDEN, P)
            for u in range(2):
                nc.vector.memset(field_x[upper, u, TILES - 1], 0.0).then_inc(pads_zeroed, 1)
            for layer in (1, 2):
                nc.vector.memset(staged[layer][upper, TILES - 1], 0.0).then_inc(pads_zeroed, 1)
            dve.wait_ge(pads_zeroed, 4)
            dve.wait_ge(w_staged[0], 32)
            nc.vector.tensor_tensor(staged[0], staged[0], w0b_staged, ALU.add).then_inc(w0_folded, 1)
            for layer in range(3):
                dve.wait_ge(w_hi_ready, layer + 1)
                for unit in LAYER[layer]:
                    if unit.split:
                        at, k = slice(0, unit.rows), HI.members.index(unit)
                        done = nc.vector.tensor_tensor(
                            w_lo[at, k, 0:unit.n], staged[layer][at, unit.t0:unit.t0 + unit.n],
                            w_hi[at, k, 0:unit.n].bitcast(F32), ALU.subtract)
                done.then_inc(w_lo_ready, 1)

            def product(s, unit):
                at, n, tiles = slice(0, unit.rows), unit.n, slice(unit.t0, unit.t0 + unit.n)
                ring, buffer, ready, freed = {
                    "N": (WHOLE, whole, whole_ready, whole_used),
                    "S": (Z, z, z_ready, z_split),
                    "D": (ZP, zp, zp_ready, zp_split)}[unit.kind]
                dst = buffer[at, ring.slot(s, unit), 0:n]
                if ring.must_wait(s, unit):
                    dve.wait_ge(freed, ring.free(s.key, unit))
                if unit.layer == 0:
                    x, h = pair_x[:, tiles], x_psum[0:ROWS0]
                elif unit.layer == 1:
                    x, h = field_x[:, s.u, tiles], hidden1[:]
                else:
                    x, h = field_x[:, 1 - s.u, tiles], hidden2[1 - s.u][:]
                h = h.unsqueeze(1).to_broadcast([unit.rows, n, COLS])
                nc.vector.tensor_tensor(dst, x, h, ALU.mult).then_inc(ready, 1)

            def low_part(s, unit):
                dve.wait_ge(hi_ready, HI.done(s.key, unit))
                if LO.must_wait(s, unit):
                    dve.wait_ge(split_used, LO.free(s.key, unit))
                at = slice(0, unit.rows)
                nc.vector.tensor_tensor(
                    z_lo[at, LO.slot(s, unit), 0:unit.n], zp[at, ZP.slot(s, unit), 0:unit.n],
                    z_hi[at, HI.slot(s, unit), 0:unit.n].bitcast(F32), ALU.subtract).then_inc(zp_split, 1)

            def sum_components(k, c, src, done, value, summed):
                dve.wait_ge(done, value)
                nc.vector.tensor_reduce(
                    out=sums[:, k, bass.ds(c * CHUNK_B, CHUNK_B)],
                    in_=src.rearrange("p (b d) -> p b d", d=DIM),
                    axis=AX.X, op=ALU.add).then_inc(summed, 1)

            def products(s, units):
                assert all(v.kind != "D" for i, u in enumerate(units) if u.kind == "D"
                           for v in units[i + 1:i + SUB_LAG + 1])
                assert all(u.kind != "D" for u in units[-SUB_LAG:])
                for i, unit in enumerate(units):
                    if unit.first and unit.layer == 0:
                        dve.wait_ge(x_in_psum, s.c + 2)
                    if unit.layer == 0 and unit.t0 in (0, UNIT):
                        dve.wait_ge(pair_x_loaded[unit.t0 // UNIT], (s.c + 2) * PAIR_X_INC)
                    if unit.first and unit.layer == 1:
                        dve.wait_ge(hidden_ready[0], s.c + 1)
                    if unit.first and unit.layer == 2:
                        dve.wait_ge(hidden_ready[1], s.c)
                    part, within = divmod(unit.t0 // UNIT, PART)
                    if unit.layer == 1 and within == 0:
                        dve.wait_ge(field_x_loaded[s.u][part], (s.turn + 1) * HALVES * 16)
                    product(s, unit)
                    if i >= SUB_LAG and units[i - SUB_LAG].kind == "D":
                        low_part(s, units[i - SUB_LAG])
                    if i == LAG[1] and s.static and s.c == 1:
                        sum_components(0, 0, direct01[:, 0], drained[1], 1, summed01)
                    if i == LAG[2] + 1 and s.has(-2):
                        sum_components(1, s.c - 2, direct2[:], drained[2], s.c - 1, summed2)
                    if s.has(0) and not (s.static and s.c == 0) and i == s.behind(LAYER[1][-1], LAG[1] + 1):
                        sum_components(0, s.c, direct01[:, s.u], drained[1], s.c + 1, summed01)

            products(BEFORE, LAYER[0])

            def step(s):
                products(s, s.units())

            run_steps(dve, step)
            sum_components(1, CHUNKS - 1, direct2[:], drained[2], CHUNKS, summed2)

        @block.tensor
        def _(pe):
            def contract(s, unit):
                at = slice(0, unit.rows)
                dst = acc_of(unit.layer, s)[:]

                def passes(w, v, tiles, start, stop):
                    for k in tiles:
                        done = nc.tensor.matmul(dst, w[at, k], v[at, k], start=start and k == 0,
                                                stop=stop and k == unit.n - 1)
                    return done

                if unit.kind == "N":
                    pe.wait_ge(whole_ready, WHOLE.done(s.key, unit))
                    w = w_whole[:, WHOLE.members.index(unit)]
                    passes(w, whole[:, WHOLE.slot(s, unit)], range(unit.n), unit.first, unit.last
                           ).then_inc(whole_used, 1)
                    return
                k, hi, lo = HI.members.index(unit), HI.slot(s, unit), LO.slot(s, unit)
                pe.wait_ge(hi_ready, HI.done(s.key, unit))
                passes(w_hi[:, k], z_hi[:, hi], range(unit.n), unit.first, False)
                passes(w_lo[:, k], z_hi[:, hi], range(unit.n), False, False)
                if unit.kind == "S":
                    pe.wait_ge(z_split, Z.done(s.key, unit))
                else:
                    pe.wait_ge(zp_split, ZP.done(s.key, unit))
                passes(w_hi[:, k], z_lo[:, lo], range(unit.n), False, False).then_inc(split_used, 1)

            pe.wait_ge(w_lo_ready, 1)
            for unit in LAYER[0]:
                contract(BEFORE, unit)
            pe.wait_ge(w_lo_ready, 3)

            def step(s):
                for unit in s.units():
                    if unit.first:
                        if unit.layer == 1:
                            pe.wait_ge(drained[0], s.c + 1)
                        elif unit.layer == 2 and s.static and s.c == CHUNKS - 1:
                            pe.wait_ge(drained[2], s.c - 1)
                        elif unit.layer == 2:
                            pe.wait_ge(drained[1], s.c + 1 if s.has(0) else s.c)
                        elif s.has(-2):
                            pe.wait_ge(drained[2], s.c - 1)
                        elif s.c == 1:
                            pe.wait_ge(drained[1], 1)
                    contract(s, unit)

            run_steps(pe, step)

            pe.wait_ge(top_loaded, TOP_LOADS * 16)
            pe.wait_ge(summed01, CHUNKS)
            pe.wait_ge(whole_ready, WHOLE.done(CHUNKS, LAYER[2][-1]))
            for m in range(TOP1 // P):
                cols = slice(m * P, (m + 1) * P)
                nc.tensor.matmul(top1_acc[m], wt1_sb[:, 0, cols], sums[:, 0], start=True, stop=False)
                nc.tensor.matmul(top1_acc[m], wt1d_sb[:, cols], dense_sb, start=False, stop=False)
            pe.wait_ge(summed2, CHUNKS)
            for m in range(TOP1 // P):
                cols = slice(m * P, (m + 1) * P)
                nc.tensor.matmul(top1_acc[m], wt1_sb[:, 1, cols], sums[:, 1], start=False, stop=True
                                 ).then_inc(top1_done, 1)
            for m in range(TOP2 // P):
                cols = slice(m * P, (m + 1) * P)
                for k in range(TOP1 // P):
                    pe.wait_ge(top1_ready, k + 1)
                    done = nc.tensor.matmul(top2_acc[m], wt2_sb[:, k, cols], top1_sb[:, k],
                                            start=(k == 0), stop=(k == TOP1 // P - 1))
                done.then_inc(top2_done, 1)
            for k in range(TOP2 // P):
                pe.wait_ge(top2_ready, k + 1)
                done = nc.tensor.matmul(y_acc, wt3_sb[:, k:k + 1], top2_sb[:, k],
                                        start=(k == 0), stop=(k == TOP2 // P - 1))
            done.then_inc(y_done, 1)


def kernel(**inputs):
    import numpy as np
    import concourse.bacc as bacc
    from concourse import mybir
    from concourse.bass_utils import run_bass_kernel_spmd as run

    def laid(a):
        return np.ascontiguousarray(a)

    a = {k: np.asarray(v) for k, v in inputs.items()}
    tables = [a[f"tbl_{f}"] for f in range(FIELDS)]
    starts = np.concatenate([[0], np.cumsum([t.shape[0] for t in tables])])[:FIELDS]

    def spread(per_row):
        padded = np.zeros((BATCH, GATHERS * LANES), np.int32)
        padded[:, :FIELDS] = per_row
        v = padded.reshape(CHUNKS, CHUNK_B, GATHERS, LANES).transpose(3, 1, 0, 2)
        return laid(v.reshape(P, CHUNKS * GATHERS))

    f = np.arange(FIELDS)
    w0 = a["L0_rec_W0"].reshape(FIELDS, FIELDS, CHANNELS)
    w0a = np.zeros((TILES0, PER_TILE, FIELDS, CHANNELS), w0.dtype)
    w0b = np.zeros_like(w0a)
    for k in range(DISTS):
        w0a[k // PER_TILE, k % PER_TILE] = w0[f, (f + k) % FIELDS]
        if k:
            w0b[k // PER_TILE, k % PER_TILE] = w0[(f + k) % FIELDS, f]
    arrays = {
        "ids": spread(a["ids"]),
        "bases": spread(np.broadcast_to(starts.astype(np.int32), (BATCH, FIELDS))),
        "table": np.concatenate(tables, axis=0),
        "w0a": laid(w0a.reshape(TILES0, ROWS0, CHANNELS).transpose(1, 0, 2)),
        "w0b": laid(w0b.reshape(TILES0, ROWS0, CHANNELS).transpose(1, 0, 2)),
        "w1": laid(a["L0_rec_W1"]),
        "w2": laid(a["L0_rec_W2"]),
        "cin_b": laid(np.stack([a["L0_rec_b0"], a["L0_rec_b1"], a["L0_rec_b2"]], axis=1)),
        "dense": laid(a["dense_ctx"].T),
        "wt1": laid(a["W_top1"]),
        "wt2": laid(a["W_top2"]),
        "wt3": laid(a["W_top3"].reshape(TOP2 // P, P).T),
        "bt1": laid(a["b_top1"].reshape(TOP1 // P, P).T),
        "bt2": laid(a["b_top2"].reshape(TOP2 // P, P).T),
    }
    nc = bacc.Bacc("TRN2", target_bir_lowering=False, num_devices=1)
    args = [nc.dram_tensor(f"in_{n}", v.shape, mybir.dt.from_np(v.dtype), kind="ExternalInput").ap()
            for n, v in arrays.items()]
    out = nc.dram_tensor("out_y", (BATCH, 1), mybir.dt.float32, kind="ExternalOutput").ap()
    build(nc, *args, out)
    r = run(nc, [{f"in_{n}": v for n, v in arrays.items()}], core_ids=[0])
    return r.results[0]["out_y"]
```
